# Optimizing a Trainium2 kernel written in Bass

```python
import numpy as np
import jax
import jax.numpy as jnp

def _softmax(x, axis=-1):
    return jax.nn.softmax(x, axis=axis)

def _gelu(x):
    return jax.nn.gelu(x, approximate=True)

def _silu(x):
    return jax.nn.silu(x)

def _sigmoid(x):
    return jax.nn.sigmoid(x)

def _layernorm(x, axis=-1, eps=1e-05):
    m = jnp.mean(x, axis=axis, keepdims=True)
    v = jnp.var(x, axis=axis, keepdims=True)
    return (x - m) / jnp.sqrt(v + eps)

def _scatter_add(tgt, idx, src, axis=0):
    return tgt.at[idx].add(src)

def _segment_sum(src, seg, n):
    return jax.ops.segment_sum(src, seg, n)
kernel_name = 'mk_cond_resid_d2_seqx_r2_6c9119'

def setup_inputs(seed: int=0):
    np.random.seed(seed)
    _w = jnp.asarray

    def _rec_inputs():
        import jax
        import jax.numpy as jnp
        _rk = jax.random.key(seed)
        x = -0.0003929 + 0.9999 * jax.random.normal(jax.random.fold_in(_rk, 1), (8, 1024, 512), jnp.float32)
        _lenS = 1024 - jax.random.randint(jax.random.fold_in(_rk, 7), (8,), 0, max(1, 1024 // 4) + 1, jnp.int32)
        _lenS2 = 1024 - jax.random.randint(jax.random.fold_in(_rk, 8), (8,), 0, max(1, 1024 // 4) + 1, jnp.int32)
        cond_1024 = 0.00386106 + 1.00199 * jax.random.normal(jax.random.fold_in(_rk, 11), (8, 512), jnp.float32)
        return (x, cond_1024)
    x, cond_1024 = _rec_inputs()

    def _L0_cond_setup():
        import jax, jax.numpy as jnp
        import numpy as np
        RANK = 8
        LN_EPS = 1e-05
        key = jax.random.key(seed)
        ks = jax.random.split(key, 8)
        B, T, D = (16, 512, 512)
        A = 512
        I = 512
        OUT = D * RANK * 4
        s = 0.02
        return {'x': jax.random.normal(ks[0], (B, T, D), jnp.float32), 'ada_emb': jax.random.normal(ks[1], (B, A), jnp.float32), 'base_up': jax.random.normal(ks[2], (D, D), jnp.float32) * s, 'base_down': jax.random.normal(ks[3], (D, D), jnp.float32) * s, 'ln_gamma': jnp.ones((A,), jnp.float32), 'ln_beta': jnp.zeros((A,), jnp.float32), 'W1': jax.random.normal(ks[4], (A, I), jnp.float32) / np.sqrt(A), 'bias1': jnp.zeros((I,), jnp.float32), 'W2': jax.random.normal(ks[5], (I, OUT), jnp.float32) / np.sqrt(I), 'bias2': jnp.zeros((OUT,), jnp.float32)}
    _L0_cond_all = _L0_cond_setup()
    _L0_cond_in = {k: v for k, v in _L0_cond_all.items() if k in ('base_up', 'base_down', 'ln_gamma', 'ln_beta', 'W1', 'bias1', 'W2', 'bias2')}
    del _L0_cond_all

    def _L1_cond_setup():
        import jax, jax.numpy as jnp
        import numpy as np
        import math
        D = 512
        H = 512
        key = jax.random.key(seed)
        k1, k2, k3, k4 = jax.random.split(key, 4)
        x = jax.random.normal(k1, (64, 256, D), dtype=jnp.float32)
        h0 = jax.random.normal(k2, (64, H), dtype=jnp.float32)
        Wx = jax.random.normal(k3, (D, 4 * H), dtype=jnp.float32) / math.sqrt(D)
        Wh = jax.random.normal(k4, (H, 4 * H), dtype=jnp.float32) / math.sqrt(H)
        b = jnp.zeros((4 * H,), dtype=jnp.float32)
        return {'x': x, 'h0': h0, 'Wx': Wx, 'Wh': Wh, 'b': b}
    _L1_cond_all = _L1_cond_setup()
    _L1_cond_in = {k: v for k, v in _L1_cond_all.items() if k in ('Wx', 'Wh', 'b')}
    del _L1_cond_all
    return {'x': x, 'cond_1024': cond_1024, 'L0_cond_base_up': _L0_cond_in['base_up'], 'L0_cond_base_down': _L0_cond_in['base_down'], 'L0_cond_ln_gamma': _L0_cond_in['ln_gamma'], 'L0_cond_ln_beta': _L0_cond_in['ln_beta'], 'L0_cond_W1': _L0_cond_in['W1'], 'L0_cond_bias1': _L0_cond_in['bias1'], 'L0_cond_W2': _L0_cond_in['W2'], 'L0_cond_bias2': _L0_cond_in['bias2'], 'L1_cond_Wx': _L1_cond_in['Wx'], 'L1_cond_Wh': _L1_cond_in['Wh'], 'L1_cond_b': _L1_cond_in['b']}

def reference(x, cond_1024, L0_cond_base_up, L0_cond_base_down, L0_cond_ln_gamma, L0_cond_ln_beta, L0_cond_W1, L0_cond_bias1, L0_cond_W2, L0_cond_bias2, L1_cond_Wx, L1_cond_Wh, L1_cond_b):
    import jax
    import jax.numpy as jnp

    def _L0_cond_ref(x, ada_emb, base_up, base_down, ln_gamma, ln_beta, W1, bias1, W2, bias2):
        import jax, jax.numpy as jnp
        import numpy as np
        RANK = 8
        LN_EPS = 1e-05
        B, T, D = x.shape
        R = RANK
        mu = jnp.mean(ada_emb, axis=-1, keepdims=True)
        var = jnp.mean(jnp.square(ada_emb - mu), axis=-1, keepdims=True)
        c = (ada_emb - mu) / jnp.sqrt(var + LN_EPS) * ln_gamma + ln_beta
        h = jax.nn.gelu(c @ W1 + bias1, approximate=False)
        w = h @ W2 + bias2
        a1, b1, a2, b2 = [t.reshape(B, D, R) for t in jnp.split(w, 4, axis=-1)]
        u = jnp.einsum('btd,bdr->btr', x, a2)
        mid = jnp.einsum('btd,dl->btl', x, base_down) + jnp.einsum('btr,blr->btl', u, b2)
        mid = jax.nn.gelu(mid, approximate=False)
        v = jnp.einsum('blr,btl->btr', b1, mid)
        out = jnp.einsum('btl,kl->btk', mid, base_up) + jnp.einsum('bkr,btr->btk', a1, v)
        return x + out

    def _L1_cond_ref(x, h0, Wx, Wh, b):
        import jax, jax.numpy as jnp
        import numpy as np
        import math
        D = 512
        H = 512
        xz = jnp.einsum('ntd,dk->ntk', x, Wx) + b
        c0 = jnp.zeros_like(h0)

        def step(carry, xz_t):
            prev_h, prev_c = carry
            z = xz_t + prev_h @ Wh
            ai, af, ao, ag = jnp.split(z, 4, axis=1)
            i = jax.nn.sigmoid(ai)
            f = jax.nn.sigmoid(af)
            o = jax.nn.sigmoid(ao)
            g = jnp.tanh(ag)
            next_c = f * prev_c + i * g
            next_h = o * jnp.tanh(next_c)
            return ((next_h, next_c), next_h)
        _, hs = jax.lax.scan(step, (h0, c0), jnp.swapaxes(xz, 0, 1))
        return jnp.swapaxes(hs, 0, 1)
    x = x + _L0_cond_ref(x, cond_1024, L0_cond_base_up, L0_cond_base_down, L0_cond_ln_gamma, L0_cond_ln_beta, L0_cond_W1, L0_cond_bias1, L0_cond_W2, L0_cond_bias2)
    x = x + _L1_cond_ref(x, cond_1024, L1_cond_Wx, L1_cond_Wh, L1_cond_b)
    return x

_drawn_inputs = setup_inputs


def setup_inputs(seed=0):
    import zlib

    import numpy as np

    out = dict(_drawn_inputs(seed))
    spreads = {'L0_cond_ln_gamma': (1.0, 0.2),
     'L0_cond_ln_beta': (0.0, 0.1),
     'L0_cond_bias1': (0.0, 0.1),
     'L0_cond_bias2': (0.0, 0.1),
     'L1_cond_b': (0.0, 0.8)}
    factors = {'L0_cond_base_up': 3.745, 'L0_cond_base_down': 3.662, 'L1_cond_Wx': 8.0, 'L1_cond_Wh': 8.0}
    for name, (base, spread) in spreads.items():
        noise = np.random.default_rng([zlib.crc32(name.encode()), seed]).standard_normal(out[name].shape)
        drawn = base * np.exp(spread * noise) if base else spread * noise
        out[name] = jnp.asarray(drawn.astype(out[name].dtype))
    for name, factor in factors.items():
        out[name] = (out[name] * factor).astype(out[name].dtype)
    return out
```

```python
from contextlib import ExitStack

import concourse.bass as bass
from concourse import mybir

ALU = mybir.AluOpType
ACT = mybir.ActivationFunctionType
F32 = mybir.dt.float32
F16 = mybir.dt.float16
U32 = mybir.dt.uint32
AX_X = mybir.AxisListType.X
RMAX = bass.bass_isa.ReduceOp.max

P = 128
LN_EPS = 1e-5

H_SCALE = 2.0 ** 15
W_TOP = 2.0 ** 14
MAX_FLOOR = 2.0 ** -40
EXPONENT_BITS = 0x7F800000


def lowrank_mixer_then_lstm(nc, x, cond, base_up, base_down, ln_gamma, ln_beta, W1, bias1,
                            W2, bias2, Wx, Wh, b, out):
    NB, T, D = x.shape
    KC = D // P
    G = Wh.shape[1] // D
    R = W2.shape[1] // D // 4
    NG4 = G * D
    TB = 64
    NBLK = T // TB
    STEPS = 4
    TURNS = TB // STEPS
    NCB = G * KC
    HB = NB // 2
    TOK = 512
    NGRP = T // TOK
    WCH = W2.shape[1] // 512
    DBL = 512 // R
    assert (NB, KC, G, R, NCB, TURNS) == (8, 4, 4, 8, 16, 16) and D == 512

    adapt_dram = nc.dram_tensor("adapt_scratch", [WCH, NB, R, DBL], F32).ap()
    x2_dram = nc.dram_tensor("x2_scratch", [NBLK, P, KC, NB, TB], F32).ap()

    def lanes(w):
        return [w[P * q:P * (q + 1), :].rearrange("(B p) n -> p B n", p=32) for q in range(KC)]

    def in_lanes(ap):
        return ap.rearrange("a (q B p) -> a q B p", q=KC, B=KC)

    def lane_view(ap):
        return ap.rearrange("a (B q p) -> a q B p", q=KC, B=KC)

    with ExitStack() as ctx:
        def sb(name, shape, dt):
            return ctx.enter_context(nc.sbuf_tensor(name, shape, dt))

        def sem(name):
            return ctx.enter_context(nc.semaphore(name))

        banks = [ctx.enter_context(nc.psum_tensor(f"bank{i}", [P, 512], F32)) for i in range(8)]

        pace = {e: sem(f"pace_{e}") for e in ("sp", "pool", "dve")}

        ident = sb("ident", [P, P], F32)
        wh_hi = sb("wh_hi", [P, KC, NG4], F16)
        wh_lo = sb("wh_lo", [P, KC, NG4], F16)
        wx_sb = sb("wx_sb", [P, KC, NG4], F32)
        bias_z = sb("bias_z", [P, NCB], F32)
        h0_z = sb("h0_z", [P, NCB, NB], F32)
        w_scale = sb("w_scale", [P, 1], F32)
        gate_scale = sb("gate_scale", [P, 1], F32)
        z_units = sb("z_units", [P, 1], F32)

        arena = sb("arena", [P, 28800], F32)
        at = [0]

        def take(parts, *dims):
            n = 1
            for d in dims:
                n *= d
            v = arena[0:parts, at[0]:at[0] + n]
            at[0] += n
            if len(dims) == 1:
                return v
            names = "abcd"[:len(dims)]
            return v.rearrange(f"z ({' '.join(names)}) -> z {' '.join(names)}", **dict(zip(names[1:], dims[1:])))

        based = take(P, KC, D)
        baseu = take(P, KC, D)
        arena_base = at[0]

        wh32 = take(P, KC, NG4)
        bup = take(P, KC, D)
        w1_sb = take(P, KC, D)
        cond_sb = take(NB, D)
        cond_l = take(NB, D)
        gam = take(NB, D)
        bet = take(NB, D)
        cn = take(NB, D)
        cT = take(P, KC, NB)
        condT = take(P, KC, NB)
        b1_sb = take(P, KC)
        brow = take(NCB, P)
        wmax = take(P, 4)
        wexp = take(P, 1)
        winv = take(P, 1)
        stats = take(NB, 6)
        mv = take(NB, 2)
        veps = take(NB, 1)
        sdev = take(NB, 1)
        rstd = take(NB, 1)
        newt = take(NB, 2)
        h0_t = take(P, 2, 8, 32)
        hidT = sb("hidT", [P, KC, NB], F32)

        ld_cond = sem("ld_cond")
        ld_small = sem("ld_small")
        ld_bias = sem("ld_bias")
        ld_w1 = sem("ld_w1")
        ld_wh = sem("ld_wh")
        ld_wx = sem("ld_wx")
        ld_bup = sem("ld_bup")
        ld_based = sem("ld_based")
        ident_zero = sem("ident_zero")
        ident_ok = sem("ident_ok")
        ln_step = sem("ln_step")
        sdev_ok = sem("sdev_ok")
        cn_ok = sem("cn_ok")
        cT_ps = sem("cT_ps")
        cT_ok = sem("cT_ok")
        condT_ps = sem("condT_ps")
        condT_ok = sem("condT_ok")
        hid_ps = sem("hid_ps")
        hid_ok = sem("hid_ok")
        bup_ps = sem("bup_ps")
        bup_ok = sem("bup_ok")
        wmax_ok = sem("wmax_ok")
        wmax_all = sem("wmax_all")
        ws_step = sem("ws_step")
        whi_ok = sem("whi_ok")
        wlo_ok = sem("wlo_ok")
        bz_ok = sem("bz_ok")
        h0_zero = sem("h0_zero")
        h0_tr = sem("h0_tr")
        cond_l_ok = sem("cond_l_ok")
        h0_ps = sem("h0_ps")
        h0_ok = sem("h0_ok")

        with nc.Block() as block:
            @block.sync
            def _(sp):
                sp.dma_start(cond_sb, cond).then_inc(ld_cond, 16)
                sp.dma_start(gam, ln_gamma.partition_broadcast(NB)).then_inc(ld_small, 16)
                sp.dma_start(bet, ln_beta.partition_broadcast(NB)).then_inc(ld_small, 16)
                sp.dma_start(w1_sb, W1.rearrange("(c p) n -> p c n", p=P)).then_inc(ld_w1, 16)
                sp.dma_start(bup, base_up.rearrange("(c p) n -> p c n", p=P)).then_inc(ld_bup, 16)
                for q, rows in enumerate(lanes(Wh)):
                    sp.dma_start(wh32[32 * q:32 * q + 32], rows).then_inc(ld_wh, 16)
                for q, rows in enumerate(lanes(Wx)):
                    sp.dma_start(wx_sb[32 * q:32 * q + 32], rows).then_inc(ld_wx, 16)
                for q, rows in enumerate(lanes(base_down)):
                    sp.dma_start(based[32 * q:32 * q + 32], rows).then_inc(ld_based, 16)
                sp.wait_ge(ld_wx, 16 * KC)
                sp.wait_ge(ld_based, 16 * KC)

            @block.gpsimd
            def _(pool):
                nc.gpsimd.memset(ident[:], 0.0).then_inc(ident_zero, 1)
                pool.wait_ge(ident_zero, 1)
                nc.gpsimd.affine_select(out=ident[:], in_=ident[:], compare_op=ALU.not_equal, fill=1.0,
                                        base=0, pattern=[[-1, P]], channel_multiplier=1).then_inc(ident_ok, 1)
                with nc.allow_non_contiguous_dma("512 bias values, once"):
                    pool.dma_start(b1_sb, bias1.rearrange("(c p) -> p c", p=P)).then_inc(ld_bias, 16)
                bv = b.rearrange("(g q h c p) -> h c g q p", g=G, q=KC, h=2, c=2)
                for h in range(2):
                    for c in range(2):
                        pool.dma_start(brow[8 * h + c:8 * h + c + 7:2, :].rearrange("g (q p) -> g q p", q=KC),
                                       bv[h, c]).then_inc(ld_bias, 16)
                pool.wait_ge(wmax_ok, 5)
                nc.gpsimd.partition_all_reduce(wexp, winv, P, RMAX).then_inc(wmax_all, 1)

            @block.vector
            def _(dve):
                nc.vector.memset(banks[2][:], 0.0)
                nc.vector.memset(banks[3][:], 0.0).then_inc(h0_zero, 1)
                dve.wait_ge(ld_cond, 16)
                nc.vector.tensor_copy(lane_view(cond_l), in_lanes(cond_sb)).then_inc(cond_l_ok, 1)
                nc.vector.bn_stats(stats, cond_sb).then_inc(ln_step, 1)
                dve.wait_ge(ln_step, 1)
                nc.vector.bn_aggr(mv, stats).then_inc(ln_step, 1)
                dve.wait_ge(ln_step, 2)
                nc.vector.tensor_scalar(veps, mv[:, 1:2], LN_EPS, None, ALU.add).then_inc(ln_step, 1)
                dve.wait_ge(sdev_ok, 1)
                nc.vector.reciprocal(rstd, sdev).then_inc(ln_step, 1)
                dve.wait_ge(ln_step, 4)
                nc.vector.tensor_scalar(newt[:, 0:1], rstd, rstd, veps, ALU.mult, ALU.mult).then_inc(ln_step, 1)
                dve.wait_ge(ln_step, 5)
                nc.vector.tensor_scalar(newt[:, 1:2], newt[:, 0:1], -0.5, 1.5, ALU.mult, ALU.add).then_inc(ln_step, 1)
                dve.wait_ge(ln_step, 6)
                nc.vector.tensor_scalar(rstd, rstd, newt[:, 1:2], None, ALU.mult).then_inc(ln_step, 1)
                dve.wait_ge(ln_step, 7)
                nc.vector.tensor_scalar(cn, cond_sb, mv[:, 0:1], rstd, ALU.subtract, ALU.mult).then_inc(ln_step, 1)
                dve.wait_ge(ln_step, 8)
                dve.wait_ge(ld_small, 16 * 2)
                nc.vector.tensor_tensor(cn, cn, gam, ALU.mult).then_inc(ln_step, 1)
                dve.wait_ge(ln_step, 9)
                nc.vector.tensor_tensor(cn, cn, bet, ALU.add).then_inc(cn_ok, 1)
                dve.wait_ge(condT_ps, 1)
                nc.vector.tensor_copy(condT, banks[1][:, 0:KC * NB].rearrange("p (c n) -> p c n", c=KC)).then_inc(condT_ok, 1)
                dve.wait_ge(cT_ps, 1)
                nc.vector.tensor_copy(cT, banks[0][:, 0:KC * NB].rearrange("p (c n) -> p c n", c=KC)).then_inc(cT_ok, 1)
                for lc in range(KC):
                    dve.wait_ge(bup_ps, lc + 1)
                    nc.vector.tensor_scalar(lane_view(baseu[:, lc, :]), in_lanes(banks[4 + lc][:]), H_SCALE, None,
                                            ALU.mult).then_inc(bup_ok, 1)
                dve.wait_ge(ld_wh, 16 * KC)
                for kb in range(KC):
                    nc.vector.tensor_reduce(wmax[:, kb:kb + 1], wh32[:, kb, :], AX_X, ALU.max,
                                            apply_absolute_value=True).then_inc(wmax_ok, 1)
                dve.wait_ge(wmax_ok, 4)
                nc.vector.tensor_reduce(winv, wmax, AX_X, ALU.max).then_inc(wmax_ok, 1)
                dve.wait_ge(wmax_all, 1)
                nc.vector.tensor_scalar(wexp, wexp, MAX_FLOOR, None, ALU.max).then_inc(ws_step, 1)
                dve.wait_ge(ws_step, 1)
                nc.vector.tensor_scalar(wexp.bitcast(U32), wexp.bitcast(U32), EXPONENT_BITS, None,
                                        ALU.bitwise_and).then_inc(ws_step, 1)
                dve.wait_ge(ws_step, 2)
                nc.vector.reciprocal(winv, wexp).then_inc(ws_step, 1)
                dve.wait_ge(ws_step, 3)
                nc.vector.tensor_scalar(w_scale[:], winv, W_TOP, None, ALU.mult).then_inc(ws_step, 1)
                nc.vector.tensor_scalar(z_units[:], winv, W_TOP * H_SCALE, None, ALU.mult).then_inc(ws_step, 1)
                nc.vector.tensor_scalar(gate_scale[:], wexp, 1.0 / (W_TOP * H_SCALE), None, ALU.mult).then_inc(ws_step, 1)
                dve.wait_ge(ws_step, 6)
                for kb in range(KC):
                    nc.vector.tensor_scalar(wh_hi[:, kb, :], wh32[:, kb, :], w_scale[:, 0:1], None,
                                            ALU.mult).then_inc(whi_ok, 1)
                for kb in range(KC):
                    dve.wait_ge(whi_ok, kb + 1)
                    nc.vector.scalar_tensor_tensor(out=wh_lo[:, kb, :], in0=wh32[:, kb, :], scalar=w_scale[:, 0:1],
                                                   in1=wh_hi[:, kb, :], op0=ALU.mult, op1=ALU.subtract).then_inc(wlo_ok, 1)
                nc.vector.tensor_scalar(bias_z[:], banks[1][:, 64:64 + NCB], z_units[:, 0:1], None, ALU.mult).then_inc(bz_ok, 1)
                dve.wait_ge(h0_ps, 1)
                for half in range(2):
                    nc.vector.transpose(h0_t[:, half].rearrange("p a b -> p (a b)"), banks[2 + half][:, 0:256]).then_inc(h0_tr, 1)
                dve.wait_ge(h0_tr, 2)
                for half in range(2):
                    nc.vector.tensor_scalar(h0_z[:, 8 * half:8 * half + 8, :], h0_t[:, half, :, 0:NB], z_units[:, 0:1], None,
                                            ALU.mult).then_inc(h0_ok, 1)

            @block.scalar
            def _(act):
                act.wait_ge(ln_step, 3)
                nc.scalar.activation(sdev, veps, ACT.Sqrt).then_inc(sdev_ok, 1)
                act.wait_ge(ld_bias, 16 * 5)
                for i in range(KC):
                    act.wait_ge(hid_ps, i + 1)
                    nc.scalar.activation(hidT[:, i, :], banks[0][:, 64 + i * NB:64 + (i + 1) * NB], ACT.Gelu,
                                         bias=b1_sb[:, i:i + 1]).then_inc(hid_ok, 1)

            @block.tensor
            def _(pe):
                pe.wait_ge(ident_ok, 1)
                pe.wait_ge(cond_l_ok, 1)
                for B in range(KC):
                    mm = nc.tensor.transpose(banks[1][:, B * NB:(B + 1) * NB], cond_l[:, B * P:(B + 1) * P], ident[0:NB, 0:NB])
                pe.wait_ge(ld_bias, 16 * 5)
                nc.tensor.transpose(banks[1][:, 64:64 + NCB], brow, ident[0:NCB, 0:NCB]).then_inc(condT_ps, 1)
                pe.wait_ge(ld_bup, 16)
                for lc in range(KC):
                    for kc in range(KC):
                        mm = nc.tensor.transpose(banks[4 + lc][:, kc * P:(kc + 1) * P], bup[:, kc, lc * P:(lc + 1) * P],
                                                 ident[:])
                    mm.then_inc(bup_ps, 1)
                pe.wait_ge(cn_ok, 1)
                for c in range(KC):
                    mm = nc.tensor.transpose(banks[0][:, c * NB:(c + 1) * NB], cn[:, c * P:(c + 1) * P], ident[0:NB, 0:NB])
                mm.then_inc(cT_ps, 1)
                pe.wait_ge(cT_ok, 1)
                pe.wait_ge(ld_w1, 16)
                for i in range(KC):
                    if i:
                        pe.wait_ge(hid_ok, i)
                    for c in range(KC):
                        mm = nc.tensor.matmul(banks[0][:, 64 + i * NB:64 + (i + 1) * NB], w1_sb[:, c, i * P:(i + 1) * P], cT[:, c, :],
                                              start=(c == 0), stop=(c == KC - 1))
                    mm.then_inc(hid_ps, 1)
                pe.wait_ge(condT_ok, 1)
                pe.wait_ge(ld_wh, 16 * KC)
                pe.wait_ge(h0_zero, 1)
                for half in range(2):
                    for kb in range(KC):
                        for q in range(KC):
                            mm = nc.tensor.matmul(
                                banks[2 + half][32 * q:32 * q + NB, 0:256], condT[:, kb, :],
                                wh32[:, kb, :].rearrange("p (g q c) -> p g q c", g=G, q=KC)[:, :, q, 64 * half:64 * half + 64],
                                start=(kb == 0), stop=(kb == KC - 1), tile_position=(0, 32 * q))
                mm.then_inc(h0_ps, 1)

        at[0] = arena_base
        NW = 4
        w2_sb = [take(P, KC, 512) for _ in range(NW)]
        b2_sb = [take(NB, 512) for _ in range(NW)]
        ad_sb = [take(NB, R, DBL) for _ in range(NW)]
        ld_w2 = [sem(f"ld_w2_{i}") for i in range(NW)]
        ad_ps = sem("ad_ps")
        ad_ok = sem("ad_ok")
        st_ad = [sem(f"st_ad_{i}") for i in range(NW)]
        w2_v = W2.rearrange("(c p) (w n) -> w p c n", p=P, n=512)
        bias2_v = bias2.rearrange("(w n) -> w n", n=512)

        with nc.Block() as block:
            @block.sync
            def _(sp):
                for i in range(NW):
                    sp.dma_start(w2_sb[i], w2_v[i]).then_inc(ld_w2[i], 16)
                    sp.dma_start(b2_sb[i], bias2_v[i].partition_broadcast(NB)).then_inc(ld_w2[i], 16)
                with sp.Fori(1, WCH // NW) as r:
                    for i in range(NW):
                        sp.wait_ge(ad_ok, (r - 1) * NW + (i + 1))
                        sp.sem_inc(pace["sp"], 1)
                        sp.dma_start(w2_sb[i], w2_v[bass.ds(r * NW + i, 1)].rearrange("a p c n -> p (a c) n")).then_inc(ld_w2[i], 16)
                        sp.dma_start(b2_sb[i], bias2_v[bass.ds(r * NW + i, 1), :].rearrange("a n -> (a n)").partition_broadcast(NB)
                                     ).then_inc(ld_w2[i], 16)

            @block.tensor
            def _(pe):
                with pe.Fori(0, WCH // NW) as r:
                    for i in range(NW):
                        pe.wait_ge(ld_w2[i], r * 32 + 32)
                        if i == 0:
                            pe.wait_ge(ad_ok, r * NW)
                        for c in range(KC):
                            mm = nc.tensor.matmul(banks[i][0:NB, :], hidT[:, c, :], w2_sb[i][:, c, :],
                                                  start=(c == 0), stop=(c == KC - 1))
                        mm.then_inc(ad_ps, 1)

            @block.vector
            def _(dve):
                with dve.Fori(0, WCH // NW) as r:
                    for i in range(NW):
                        dve.wait_ge(ad_ps, r * NW + (i + 1))
                        dve.wait_ge(st_ad[i], r * 16)
                        nc.vector.tensor_tensor(ad_sb[i].rearrange("b r d -> b d r"),
                                                banks[i][0:NB, :].rearrange("b (d r) -> b d r", r=R),
                                                b2_sb[i].rearrange("b (d r) -> b d r", r=R), ALU.add).then_inc(ad_ok, 1)

            @block.scalar
            def _(act):
                with act.Fori(0, WCH // NW) as r:
                    for i in range(NW):
                        act.wait_ge(ad_ok, r * NW + (i + 1))
                        act.dma_start(adapt_dram[bass.ds(r * NW + i, 1)].rearrange("a b r d -> (a b) r d"),
                                      ad_sb[i]).then_inc(st_ad[i], 16)
                for i in range(NW):
                    act.wait_ge(st_ad[i], 16 * WCH // NW)

        at[0] = arena_base
        xn = [take(P, TOK // P, D) for _ in range(2)]
        xl = [take(P, TOK // P, D) for _ in range(2)]
        xT = [take(P, KC, TOK) for _ in range(2)]
        midT = take(P, KC, TOK)
        x2o = [take(P, KC, TOK) for _ in range(2)]
        wd = take(P, KC, D)
        wu = take(P, KC, D)
        lr = take(R, 4, D)
        NQ = NB * NGRP
        ld_x = [sem("ld_x0"), sem("ld_x1")]
        ld_lr = sem("ld_lr")
        wform_ps = sem("wform_ps")
        wform_ok = sem("wform_ok")
        xl_ok = sem("xl_ok")
        xT_ps = sem("xT_ps")
        xT_ok = sem("xT_ok")
        mid_ps = sem("mid_ps")
        mid_ok = sem("mid_ok")
        out_ps = sem("out_ps")
        x2_ok = sem("x2_ok")
        st_x2 = [sem("st_x2_0"), sem("st_x2_1")]
        form_bank, xT_bank, mid_bank, out_bank = banks[0:2], banks[2:4], banks[4:6], banks[6:8]

        with nc.Block() as block:
            @block.sync
            def _(sp):
                LR_DMAS = 2 + 2 * KC
                BPG = TOK // TB
                ad_v = adapt_dram.rearrange("(j q h) b r (c p) -> j h c b r q p", j=4, q=KC, c=2)

                def load_factors(bt):
                    for j in (1, 3):
                        sp.dma_start(lr[:, j, :].rearrange("r (w d) -> r w d", d=DBL),
                                     adapt_dram[8 * j:8 * j + 8, bass.ds(bt, 1)].rearrange("w b r d -> r (w b) d")
                                     ).then_inc(ld_lr, 16)
                    for j in (0, 2):
                        for B in range(KC):
                            sp.dma_start(lr[:, j, B * P:(B + 1) * P].rearrange("r (q p) -> r q p", q=KC),
                                         ad_v[j, B // 2, B % 2, bass.ds(bt, 1)].rearrange("b r q p -> (b r) q p")
                                         ).then_inc(ld_lr, 16)

                def load_x(bt, g):
                    sp.dma_start(xn[g], x[bass.ds(bt, 1), g * TOK:(g + 1) * TOK, :].rearrange(
                        "b (t p) d -> p (b t) d", p=P)).then_inc(ld_x[g], 16)

                def store_x2(bt, g):
                    for B in range(KC):
                        sp.wait_ge(x2_ok, bt * (NGRP * KC) + (g * KC + B + 1))
                        sp.sem_inc(pace["sp"], 1)
                        sp.dma_start(
                            x2_dram[g * BPG:(g + 1) * BPG, :, B, bass.ds(bt, 1), :].rearrange("k p b t -> p (k b) t"),
                            x2o[g][:, B, :].rearrange("p (k t) -> p k t", t=TB)).then_inc(st_x2[g], 16)

                load_factors(0)
                for g in range(NGRP):
                    load_x(0, g)
                with sp.Fori(0, NB - 1) as bt:
                    for g in range(NGRP):
                        sp.wait_ge(xl_ok, bt * NGRP + (g + 1))
                        sp.sem_inc(pace["sp"], 1)
                        load_x(bt + 1, g)
                        store_x2(bt, g)
                    sp.wait_ge(wform_ok, bt * (2 * KC) + 2 * KC)
                    sp.sem_inc(pace["sp"], 1)
                    load_factors(bt + 1)
                for g in range(NGRP):
                    store_x2(NB - 1, g)
                for g in range(NGRP):
                    sp.wait_ge(st_x2[g], 16 * KC * NB)

            @block.tensor
            def _(pe):
                with pe.Fori(0, NB) as bt:
                    pe.wait_ge(ld_lr, bt * 160 + 160)
                    for i in range(2 * KC):
                        if i >= 2:
                            pe.wait_ge(wform_ok, bt * (2 * KC) + (i - 1))
                        else:
                            pe.wait_ge(wform_ok, bt * (2 * KC))
                        lhsT = lr[:, 2, i * P:(i + 1) * P] if i < KC else lr[:, 1, (i - KC) * P:(i - KC + 1) * P]
                        nc.tensor.matmul(form_bank[i % 2][:], lhsT, lr[:, 3 if i < KC else 0, :],
                                         start=True, stop=True).then_inc(wform_ps, 1)
                    for g in range(NGRP):
                        pe.wait_ge(xl_ok, bt * NGRP + (g + 1))
                        for B in range(KC):
                            n = g * KC + B
                            pe.wait_ge(xT_ok, bt * (NGRP * KC) + max(n - 1, 0))
                            for tt in range(TOK // P):
                                mm = nc.tensor.transpose(xT_bank[n % 2][:, tt * P:(tt + 1) * P],
                                                         xl[g][:, tt, B * P:(B + 1) * P], ident[:])
                            mm.then_inc(xT_ps, 1)
                        pe.wait_ge(xT_ok, bt * (NGRP * KC) + (g + 1) * KC)
                        pe.wait_ge(wform_ok, (bt + 1) * (2 * KC))
                        for lc in range(KC):
                            n = g * KC + lc
                            pe.wait_ge(mid_ok, bt * (NGRP * KC) + max(n - 1, 0))
                            for B in range(KC):
                                mm = nc.tensor.matmul(mid_bank[n % 2][:], wd[:, B, lc * P:(lc + 1) * P], xT[g][:, B, :],
                                                      start=(B == 0), stop=(B == KC - 1))
                            mm.then_inc(mid_ps, 1)
                        pe.wait_ge(mid_ok, bt * (NGRP * KC) + (g + 1) * KC)
                        for B in range(KC):
                            n = g * KC + B
                            pe.wait_ge(x2_ok, bt * (NGRP * KC) + max(n - 1, 0))
                            for lc in range(KC):
                                mm = nc.tensor.matmul(out_bank[n % 2][:], wu[:, lc, B * P:(B + 1) * P], midT[:, lc, :],
                                                      start=(lc == 0), stop=(lc == KC - 1))
                            mm.then_inc(out_ps, 1)

            @block.scalar
            def _(act):
                with act.Fori(0, NB) as bt:
                    for g in range(NGRP):
                        for lc in range(KC):
                            n = g * KC + lc
                            act.wait_ge(mid_ps, bt * (NGRP * KC) + (n + 1))
                            if lc == 0:
                                act.wait_ge(out_ps, bt * (NGRP * KC) + g * KC)
                            nc.scalar.activation(midT[:, lc, :], mid_bank[n % 2][:], ACT.Gelu).then_inc(mid_ok, 1)

            @block.vector
            def _(dve):
                with dve.Fori(0, NB) as bt:
                    dve.wait_ge(out_ps, bt * (NGRP * KC))
                    for i in range(2 * KC):
                        dve.wait_ge(wform_ps, bt * (2 * KC) + (i + 1))
                        if i < KC:
                            nc.vector.tensor_tensor(wd[:, i, :], form_bank[i % 2][:], based[:, i, :],
                                                    ALU.add).then_inc(wform_ok, 1)
                        else:
                            nc.vector.scalar_tensor_tensor(out=wu[:, i - KC, :], in0=form_bank[i % 2][:], scalar=H_SCALE,
                                                           in1=baseu[:, i - KC, :], op0=ALU.mult,
                                                           op1=ALU.add).then_inc(wform_ok, 1)
                    for g in range(NGRP):
                        for B in range(KC):
                            n = g * KC + B
                            dve.wait_ge(xT_ps, bt * (NGRP * KC) + (n + 1))
                            nc.vector.tensor_copy(xT[g][:, B, :], xT_bank[n % 2][:]).then_inc(xT_ok, 1)
                        dve.wait_ge(st_x2[g], bt * (16 * KC))
                        for B in range(KC):
                            n = g * KC + B
                            dve.wait_ge(out_ps, bt * (NGRP * KC) + (n + 1))
                            nc.vector.scalar_tensor_tensor(out=x2o[g][:, B, :], in0=xT[g][:, B, :], scalar=2.0 * H_SCALE,
                                                           in1=out_bank[n % 2][:], op0=ALU.mult,
                                                           op1=ALU.add).then_inc(x2_ok, 1)

            @block.gpsimd
            def _(pool):
                with pool.Fori(0, NB) as bt:
                    for g in range(NGRP):
                        pool.wait_ge(ld_x[g], bt * 16 + 16)
                        pool.wait_ge(xT_ps, bt * (NGRP * KC))
                        pool.sem_inc(pace["pool"], 1)
                        for tt in range(TOK // P):
                            cp = nc.gpsimd.tensor_copy(lane_view(xl[g][:, tt, :]), in_lanes(xn[g][:, tt, :]))
                        cp.then_inc(xl_ok, 1)

        at[0] = 0
        XS = 4
        xz = take(P, NCB, NB, 2 * TB)
        x2s = take(P, XS * KC, NB * TB)
        hs = take(P, KC, NB, 2 * TB)
        wx_st = sb("wx_st", [P, KC, P], F32)
        y_t = sb("y_t", [P, P], F32)
        y_n = sb("y_n", [P, KC, 32], F32)
        h_st = sb("h_st", [P, 2, KC, 2 * NB], F16)
        zt = [sb(f"zt{i}", [P, 8, 32], F32) for i in range(2)]
        u = [sb(f"u{i}", [P, 8, NB], F32) for i in range(2)]
        z = [sb(f"z{i}", [P, 8, NB], F32) for i in range(2)]
        gt = [sb(f"gt{i}", [P, 8, NB], F32) for i in range(2)]
        fc = [sb(f"fc{i}", [P, 2, NB], F32) for i in range(2)]
        ig = [sb(f"ig{i}", [P, 2, NB], F32) for i in range(2)]
        cell = [sb(f"cell{i}", [P, 2, NB], F32) for i in range(2)]
        tc = [sb(f"tc{i}", [P, 2, NB], F32) for i in range(2)]

        def pair(name):
            return [sem(f"{name}0"), sem(f"{name}1")]

        state_ok = sem("state_ok")
        z_ps = pair("z_ps")
        zt_ok = pair("zt_ok")
        u_ok = pair("u_ok")
        z_ok = pair("z_ok")
        sig_ok = pair("sig_ok")
        tanh_ok = pair("tanh_ok")
        ig_ok = pair("ig_ok")
        cell_ok = pair("cell_ok")
        tc_ok = pair("tc_ok")
        h32_ok = pair("h32_ok")
        h_ok = pair("h_ok")
        wx_ok = sem("wx_ok")
        proj_ps = pair("proj_ps")
        proj_ok = pair("proj_ok")
        wx_used = [sem(f"wx_used{i}") for i in range(KC - 1)] + [proj_ps[1]]
        h0_in = sem("h0_in")
        ld_x2 = sem("ld_x2")
        y_add = sem("y_add")
        y_ps = sem("y_ps")
        y_ok = sem("y_ok")
        st_y = sem("st_y")

        z_bank = [[banks[0], banks[1]], [banks[2], banks[3]]]
        proj_bank = [banks[4], banks[5]]
        y_bank = banks[6]
        wh_v = [w[:].rearrange("p k (g q c) -> p k g q c", g=G, q=KC) for w in (wh_hi, wh_lo)]
        wx_v = wx_sb[:].rearrange("p k (g q h c l) -> p k h c g q l", g=G, q=KC, h=2, c=2)
        out_v = out.rearrange("(g b) (n t) (q B p) -> n g B b t q p", b=2, t=TB, q=KC, B=KC)

        with nc.Block() as block:
            def turns(eng, body):
                with eng.Fori(0, TURNS) as j:
                    body(eng, 0, j, True, False)
                with eng.Fori(1, NBLK - 1) as n:
                    with eng.Fori(0, TURNS) as j:
                        body(eng, n, j, True, True)
                with eng.Fori(0, TURNS) as j:
                    body(eng, NBLK - 1, j, False, True)

            @block.sync
            def _(sp):
                def load(n):
                    sp.dma_start(x2s[:, bass.ds((n & (XS - 1)) * KC, KC), :],
                                 x2_dram[bass.ds(n, 1)].rearrange("n p c b t -> p (n c) (b t)")).then_inc(ld_x2, 16)

                def store(n, j):
                    sp.wait_ge(y_ok, (n - 1) * TURNS + j + 1)
                    sp.sem_inc(pace["sp"], 1)
                    for bb in range(2):
                        sp.dma_start(out_v[bass.ds(n - 1, 1), bass.ds(j & 3, 1), bass.ds((j >> 2).with_bounds(min_val=0, max_val=KC - 1), 1), bb].rearrange(
                            "n g B t q p -> (n g B t) q p"), y_n[64 * bb:64 * bb + 64]).then_inc(st_y, 16)

                sp.dma_start(x2s[:, 0:KC, :], x2_dram[0].rearrange("p c b t -> p c (b t)")).then_inc(ld_x2, 16)
                sp.wait_ge(ld_x2, 16)
                sp.dma_start(x2s[:, KC:2 * KC, :], x2_dram[1].rearrange("p c b t -> p c (b t)")).then_inc(ld_x2, 16)
                sp.wait_ge(ld_x2, 32)
                sp.dma_start(x2s[:, 2 * KC:3 * KC, :], x2_dram[2].rearrange("p c b t -> p c (b t)")).then_inc(ld_x2, 16)
                with sp.Fori(1, NBLK - 2) as n:
                    sp.wait_ge(ld_x2, n * 16 + 32)
                    sp.wait_ge(y_add, (n - 1) * TURNS)
                    sp.sem_inc(pace["sp"], 1)
                    load(n + 2)
                    with sp.Fori(0, TURNS) as j:
                        store(n, j)
                with sp.Fori(NBLK - 2, NBLK + 1) as n:
                    with sp.Fori(0, TURNS) as j:
                        store(n, j)
                sp.wait_ge(st_y, 32 * NBLK * TURNS)

            @block.gpsimd
            def _(pool):
                def stage(done, j, kb):
                    pool.wait_ge(wx_used[kb], done)
                    pool.sem_inc(pace["pool"], 1)
                    nc.gpsimd.tensor_copy(
                        wx_st[:, kb, :].rearrange("p (q l) -> p q l", q=KC),
                        wx_cols(kb, j)).then_inc(wx_ok, 1)

                def wx_cols(kb, j):
                    v = wx_sb[:, kb, :].rearrange("p (g q h l) -> p g q h l", g=G, q=KC, h=4)
                    return v[:, bass.ds((j >> 1) & 3, 1), :, bass.ds((j >> 3).with_bounds(min_val=0, max_val=1) * 2 + (j & 1), 1), :].rearrange(
                        "p g q h l -> p (g q) (h l)")

                def y_sum(n, j):
                    pool.wait_ge(y_ps, (n - 1) * TURNS + j)
                    nc.gpsimd.tensor_tensor(
                        y_t[:].rearrange("p (b t) -> p b t", b=2),
                        hs.rearrange("p c b t -> p (c b) t")[:, bass.ds(j * 2, 2), bass.ds(((n - 1) & 1) * TB, TB)],
                        x2s.rearrange("p c (b t) -> p (c b) t", t=TB)[
                            :, bass.ds(((n - 1) & (XS - 1)) * (KC * NB) + j * 2, 2), :],
                        ALU.add).then_inc(y_add, 1)

                with pool.Fori(0, TURNS) as j:
                    for kb in range(KC):
                        stage(j, j, kb)

                def turn(eng, n, j, project, output):
                    if output:
                        y_sum(n, j)
                    if project:
                        for kb in range(KC):
                            stage((n + 1) * TURNS + j, j, kb)

                with pool.Fori(0, TURNS) as j:
                    turn(pool, 0, j, True, False)
                with pool.Fori(1, NBLK - 1) as n:
                    pool.wait_ge(h_ok[0], n * TB + 1)
                    pool.wait_ge(h_ok[1], n * TB + 1)
                    pool.sem_inc(pace["pool"], 1)
                    with pool.Fori(0, TURNS) as j:
                        turn(pool, n, j, True, True)
                with pool.Fori(NBLK - 1, NBLK + 1) as n:
                    pool.wait_ge(h_ok[0], n * TB + 1)
                    pool.wait_ge(h_ok[1], n * TB + 1)
                    pool.sem_inc(pace["pool"], 1)
                    with pool.Fori(0, TURNS) as j:
                        turn(pool, n, j, False, True)

            @block.tensor
            def _(pe):
                def project(n_next, j, hb, kb):
                    row = (n_next & (XS - 1)) * KC + kb
                    mm = nc.tensor.matmul(proj_bank[hb][:, 0:HB * TB], wx_st[:, kb, :],
                                          x2s[:, bass.ds(row, 1), hb * HB * TB:(hb + 1) * HB * TB].rearrange("p a t -> p (a t)"),
                                          start=(kb == 0), stop=(kb == KC - 1))
                    return mm

                def recur(parity, k_half, n_half, chunks, start=False, stop=False):
                    for kb in chunks:
                        for part in range(2):
                            for q in range(KC):
                                mm = nc.tensor.matmul(
                                    z_bank[n_half][parity][32 * q:32 * q + 2 * NB, 0:256], h_st[:, parity, kb, :],
                                    wh_v[part][:, kb, :, q, 64 * n_half:64 * n_half + 64],
                                    start=(start and part == 0), stop=(stop and part == 1), tile_position=(0, 32 * q))
                        start, stop = False, stop
                    return mm

                pe.wait_ge(ld_x2, 16)
                pe.wait_ge(state_ok, 5)
                with pe.Fori(0, TURNS) as j:
                    for kb in range(KC):
                        pe.wait_ge(wx_ok, j * KC + (kb + 1))
                        for hb in range(2):
                            if kb == 0:
                                pe.wait_ge(proj_ok[hb], j)
                            mm = project(0, j, hb, kb)
                            if kb == KC - 1 and hb == 0:
                                mm.then_inc(proj_ps[0], 1)
                        mm.then_inc(wx_used[kb], 1)

                def turn(eng, n, j, with_projection, with_output):
                    done = (n + 1) * TURNS + j
                    if with_output:
                        done_y = (n - 1) * TURNS + j
                    for s in range(STEPS):
                        t = n * TB + j * STEPS + s
                        par = s & 1
                        if with_projection:
                            if s == 0:
                                pe.wait_ge(ld_x2, (n + 2) * 16)
                            pe.wait_ge(wx_ok, done * KC + (s + 1))
                            for hb in range(2):
                                if s == 0:
                                    pe.wait_ge(proj_ok[hb], done)
                                mm = project(n + 1, j, hb, s)
                                if s == KC - 1 and hb == 0:
                                    mm.then_inc(proj_ps[0], 1)
                            mm.then_inc(wx_used[s], 1)
                        if with_output and s == 1:
                            pe.wait_ge(y_add, done_y + 1)
                            pe.wait_ge(y_ok, done_y)
                            nc.tensor.transpose(y_bank[:, 0:P], y_t[:], ident[:]).then_inc(y_ps, 1)
                        pe.wait_ge(h_ok[0], t + 1)
                        recur(par, 0, 0, (0, 1), start=True)
                        recur(par, 0, 1, (0,), start=True)
                        pe.wait_ge(h_ok[1], t + 1)
                        recur(par, 1, 0, (2,))
                        recur(par, 1, 0, (3,), stop=True).then_inc(z_ps[0], 1)
                        recur(par, 0, 1, (1,))
                        recur(par, 1, 1, (2,))
                        recur(par, 1, 1, (3,), stop=True).then_inc(z_ps[1], 1)

                turns(pe, turn)
                with pe.Fori(0, TURNS) as j:
                    pe.wait_ge(y_add, j + ((NBLK - 1) * TURNS + 1))
                    pe.wait_ge(y_ok, j + (NBLK - 1) * TURNS)
                    nc.tensor.transpose(y_bank[:, 0:P], y_t[:], ident[:]).then_inc(y_ps, 1)

            @block.scalar
            def _(act):
                gate_s = act.alloc_register("gate_s")
                proj_s = act.alloc_register("proj_s")
                act.reg_load(gate_s, gate_scale[0:1, 0:1].bitcast(U32))
                act.reg_load(proj_s, w_scale[0:1, 0:1].bitcast(U32))

                def take_projection(n_next, j, hb):
                    act.wait_ge(proj_ps[hb], n_next * TURNS + j + 1)
                    nc.scalar.activation(
                        xz[:, bass.ds(j, 1), hb * HB:(hb + 1) * HB, bass.ds((n_next & 1) * TB, TB)].rearrange(
                            "p a b t -> p (a b) t"),
                        proj_bank[hb][:, 0:HB * TB].rearrange("p (b t) -> p b t", b=HB), ACT.Identity,
                        bias=bias_z[:, bass.ds(j, 1)], scale=proj_s).then_inc(proj_ok[hb], 1)

                def take_output(count):
                    act.wait_ge(y_ps, count)
                    act.wait_ge(st_y, (count - 1) * 32)
                    nc.scalar.activation(y_n[:], y_bank[:, 0:P].rearrange("p (q l) -> p q l", q=KC), ACT.Copy,
                                         scale=1.0 / H_SCALE).then_inc(y_ok, 1)

                nc.scalar.activation(tc[0][:, 0, 0:1], gate_scale[:], ACT.Sigmoid)
                with act.Fori(0, TURNS) as j:
                    for hb in range(2):
                        take_projection(0, j, hb)

                def turn(eng, n, j, with_projection, with_output):
                    for s in range(STEPS):
                        t = n * TB + j * STEPS + s
                        if with_projection and s == STEPS - 1:
                            for hb in range(2):
                                take_projection(n + 1, j, hb)
                        if with_output and s == 1:
                            take_output((n - 1) * TURNS + j + 1)
                        for half in range(2):
                            act.wait_ge(z_ok[half], t + 1)
                            nc.scalar.activation(gt[half][:, 0:6, :], z[half][:, 0:6, :], ACT.Sigmoid,
                                                 scale=gate_s).then_inc(sig_ok[half], 1)
                            nc.scalar.activation(gt[half][:, 6:8, :], z[half][:, 6:8, :], ACT.Tanh,
                                                 scale=gate_s).then_inc(tanh_ok[half], 1)
                            act.wait_ge(cell_ok[half], t + 1)
                            nc.scalar.activation(tc[half][:], cell[half][:], ACT.Tanh).then_inc(tc_ok[half], 1)

                turns(act, turn)
                with act.Fori(0, TURNS) as j:
                    take_output(j + ((NBLK - 1) * TURNS + 1))

            @block.vector
            def _(dve):
                nc.vector.memset(h_st[:], 0.0).then_inc(state_ok, 1)
                for half in range(2):
                    for par in range(2):
                        nc.vector.memset(z_bank[half][par][:], 0.0).then_inc(state_ok, 1)
                    nc.vector.memset(cell[half][:], 0.0).then_inc(h_ok[half], 1)
                dve.wait_ge(proj_ok[0], TURNS)
                dve.wait_ge(proj_ok[1], TURNS)
                nc.vector.tensor_tensor(xz[:, :, :, 0], xz[:, :, :, 0], h0_z[:], ALU.add).then_inc(h0_in, 1)
                dve.wait_ge(h0_in, 1)

                def to_lanes(half, par, t):
                    dve.wait_ge(z_ps[half], t + 1)
                    nc.vector.transpose(zt[half][:].rearrange("p a b -> p (a b)"),
                                        z_bank[half][par][:, 0:256]).then_inc(zt_ok[half], 1)

                def add_projection(half, pos, t):
                    dve.wait_ge(zt_ok[half], t + 1)
                    nc.vector.tensor_tensor(u[half][:], zt[half][:, :, 0:NB],
                                            xz[:, 8 * half:8 * half + 8, :, bass.ds(pos, 1)].rearrange(
                                                "p a b t -> p a (b t)"), ALU.add).then_inc(u_ok[half], 1)

                def add_low(half, t):
                    dve.wait_ge(u_ok[half], t + 1)
                    nc.vector.tensor_tensor(z[half][:], zt[half][:, :, NB:2 * NB], u[half][:],
                                            ALU.add).then_inc(z_ok[half], 1)

                def keep_part(half, t):
                    dve.wait_ge(sig_ok[half], t + 1)
                    nc.vector.tensor_tensor(fc[half][:], gt[half][:, 2:4, :], cell[half][:], ALU.mult)

                def input_part(half, t):
                    dve.wait_ge(tanh_ok[half], t + 1)
                    nc.vector.tensor_tensor(ig[half][:], gt[half][:, 0:2, :], gt[half][:, 6:8, :],
                                            ALU.mult).then_inc(ig_ok[half], 1)

                def new_cell(half, t):
                    dve.wait_ge(ig_ok[half], t + 1)
                    nc.vector.tensor_tensor(cell[half][:], fc[half][:], ig[half][:], ALU.add).then_inc(cell_ok[half], 1)

                def new_h(half, nxt, pos, t):
                    ch = slice(2 * half, 2 * half + 2)
                    dve.wait_ge(tc_ok[half], t + 1)
                    nc.vector.scalar_tensor_tensor(out=h_st[:, nxt, ch, 0:NB], in0=gt[half][:, 4:6, :],
                                                   scalar=H_SCALE, in1=tc[half][:], op0=ALU.mult, op1=ALU.mult)
                    nc.vector.scalar_tensor_tensor(out=h32(half, pos), in0=gt[half][:, 4:6, :], scalar=H_SCALE,
                                                   in1=tc[half][:], op0=ALU.mult, op1=ALU.mult).then_inc(h32_ok[half], 1)

                def h32(half, pos):
                    return hs[:, 2 * half:2 * half + 2, :, bass.ds(pos, 1)].rearrange("p c b t -> p c (b t)")

                def h_rest(half, nxt, pos, t):
                    ch = slice(2 * half, 2 * half + 2)
                    dve.wait_ge(h32_ok[half], t + 1)
                    nc.vector.tensor_tensor(h_st[:, nxt, ch, NB:2 * NB], h32(half, pos), h_st[:, nxt, ch, 0:NB],
                                            ALU.subtract).then_inc(h_ok[half], 1)

                def turn(eng, n, j, with_projection, with_output):
                    for s in range(STEPS):
                        t = n * TB + j * STEPS + s
                        pos = (n & 1) * TB + j * STEPS + s
                        nxt = 1 - (s & 1)
                        to_lanes(0, s & 1, t)
                        add_projection(0, pos, t)
                        add_low(0, t)
                        to_lanes(1, s & 1, t)
                        keep_part(0, t)
                        input_part(0, t)
                        add_projection(1, pos, t)
                        new_cell(0, t)
                        add_low(1, t)
                        new_h(0, nxt, pos, t)
                        keep_part(1, t)
                        h_rest(0, nxt, pos, t)
                        input_part(1, t)
                        new_cell(1, t)
                        new_h(1, nxt, pos, t)
                        h_rest(1, nxt, pos, t)

                def start_block(n):
                    dve.wait_ge(proj_ok[0], (n + 1) * TURNS)
                    dve.wait_ge(proj_ok[1], (n + 1) * TURNS)

                with dve.Fori(0, TURNS) as j:
                    turn(dve, 0, j, True, False)
                with dve.Fori(1, NBLK - 1) as n:
                    start_block(n)
                    dve.wait_ge(y_add, (n - 1) * TURNS)
                    dve.sem_inc(pace["dve"], 1)
                    with dve.Fori(0, TURNS) as j:
                        turn(dve, n, j, True, True)
                start_block(NBLK - 1)
                dve.wait_ge(y_add, (NBLK - 2) * TURNS)
                with dve.Fori(0, TURNS) as j:
                    turn(dve, NBLK - 1, j, False, True)


_INS = ['x', 'cond_1024', 'L0_cond_base_up', 'L0_cond_base_down', 'L0_cond_ln_gamma', 'L0_cond_ln_beta',
        'L0_cond_W1', 'L0_cond_bias1', 'L0_cond_W2', 'L0_cond_bias2', 'L1_cond_Wx', 'L1_cond_Wh', 'L1_cond_b']
_OUTS = [((8, 1024, 512), 'float32')]


def kernel(**inputs):
    import numpy as _np
    import concourse.bacc as _bacc
    from concourse import mybir as _mybir
    from concourse.bass_utils import run_bass_kernel_spmd as _run

    nc = _bacc.Bacc("TRN2", target_bir_lowering=False, num_devices=1)
    arrays, args = {}, []
    for name in _INS:
        a = _np.ascontiguousarray(inputs[name])
        arrays[f"in_{name}_dram"] = a
        args.append(nc.dram_tensor(f"in_{name}_dram", a.shape, _mybir.dt.from_np(a.dtype), kind="ExternalInput").ap())
    for i, (shape, dtype) in enumerate(_OUTS):
        dt = _mybir.dt.from_np(_np.dtype(dtype))
        args.append(nc.dram_tensor(f"out_{i}_dram", shape, dt, kind="ExternalOutput").ap())
    lowrank_mixer_then_lstm(nc, *args)
    r = _run(nc, [arrays], core_ids=[0])
    got = tuple(r.results[0][f"out_{i}_dram"] for i in range(len(_OUTS)))
    return got[0]
```

```python
from contextlib import ExitStack

import concourse.bass as bass
from concourse import mybir

ALU = mybir.AluOpType
ACT = mybir.ActivationFunctionType
F32 = mybir.dt.float32
F16 = mybir.dt.float16
U32 = mybir.dt.uint32
AX_X = mybir.AxisListType.X
RMAX = bass.bass_isa.ReduceOp.max

P = 128
LN_EPS = 1e-5

H_SCALE = 2.0 ** 15
W_TOP = 2.0 ** 14
MAX_FLOOR = 2.0 ** -40
EXPONENT_BITS = 0x7F800000


def lowrank_mixer_then_lstm(nc, x, cond, base_up, base_down, ln_gamma, ln_beta, W1, bias1,
                            W2, bias2, Wx, Wh, b, out):
    NB, T, D = x.shape
    KC = D // P
    G = Wh.shape[1] // D
    R = W2.shape[1] // D // 4
    NG4 = G * D
    TB = 32
    NBLK = T // TB
    NCB = G * KC
    TOK = NB * TB
    TT = TOK // P
    BPT = NB // TT
    WCH = W2.shape[1] // 512
    DBL = 512 // R
    BR = NB * R
    assert (NB, KC, G, R, NCB, TT) == (8, 4, 4, 8, 16, 2) and D == 512

    adapt_dram = nc.dram_tensor("adapt_scratch", [WCH, NB, R, DBL], F32).ap()

    def lanes(w):
        return [w[P * q:P * (q + 1), :].rearrange("(B p) n -> p B n", p=32) for q in range(KC)]

    def in_lanes(ap):
        return ap.rearrange("a (q B p) -> a q B p", q=KC, B=KC)

    def lane_view(ap):
        return ap.rearrange("a (B q p) -> a q B p", q=KC, B=KC)

    with ExitStack() as ctx:
        def sb(name, shape, dt):
            return ctx.enter_context(nc.sbuf_tensor(name, shape, dt))

        def sem(name):
            return ctx.enter_context(nc.semaphore(name))

        banks = [ctx.enter_context(nc.psum_tensor(f"bank{i}", [P, 512], F32)) for i in range(8)]

        pace = {e: sem(f"pace_{e}") for e in ("sp", "pool", "dve")}

        ident = sb("ident", [P, P], F32)
        wh_hi = sb("wh_hi", [P, KC, NG4], F16)
        wh_lo = sb("wh_lo", [P, KC, NG4], F16)
        wx_l = sb("wx_l", [P, KC, NCB, P], F32)
        based = sb("based", [P, KC, D], F32)
        baseu = sb("baseu", [P, KC, D], F32)
        a2_c = sb("a2_c", [P, KC, BR], F32)
        b1_c = sb("b1_c", [P, KC, BR], F32)
        b2_t = sb("b2_t", [BR, D], F32)
        a1_t = sb("a1_t", [BR, D], F32)
        own = sb("own", [BR, NB, TB], F32)
        bias_z = sb("bias_z", [P, NCB], F32)
        h0_z = sb("h0_z", [P, NCB, NB], F32)
        w_scale = sb("w_scale", [P, 1], F32)
        w_scale_h = sb("w_scale_h", [P, 1], F32)
        gate_scale = sb("gate_scale", [P, 1], F32)
        z_units = sb("z_units", [P, 1], F32)

        arena = sb("arena", [P, 24200], F32)
        at = [0]

        def take(parts, *dims):
            n = 1
            for d in dims:
                n *= d
            v = arena[0:parts, at[0]:at[0] + n]
            at[0] += n
            if len(dims) == 1:
                return v
            names = "abcd"[:len(dims)]
            return v.rearrange(f"z ({' '.join(names)}) -> z {' '.join(names)}", **dict(zip(names[1:], dims[1:])))

        wh32 = take(P, KC, NG4)
        wx32 = take(P, KC, NG4)
        bup = take(P, KC, D)
        w1_sb = take(P, KC, D)
        cond_sb = take(NB, D)
        cond_l = take(NB, D)
        gam = take(NB, D)
        bet = take(NB, D)
        cn = take(NB, D)
        cT = take(P, KC, NB)
        condT = take(P, KC, NB)
        b1_sb = take(P, KC)
        brow = take(NCB, P)
        wmax = take(P, 4)
        wexp = take(P, 1)
        winv = take(P, 1)
        stats = take(NB, 6)
        mv = take(NB, 2)
        veps = take(NB, 1)
        sdev = take(NB, 1)
        rstd = take(NB, 1)
        newt = take(NB, 2)
        h0_t = take(P, 2, 8, 32)
        hidT = sb("hidT", [P, KC, NB], F32)

        ld_cond = sem("ld_cond")
        ld_small = sem("ld_small")
        ld_bias = sem("ld_bias")
        ld_w1 = sem("ld_w1")
        ld_wh = sem("ld_wh")
        ld_wx = sem("ld_wx")
        ld_bup = sem("ld_bup")
        ld_based = sem("ld_based")
        ident_zero = sem("ident_zero")
        ident_ok = sem("ident_ok")
        own_step = sem("own_step")
        wx_ok = sem("wx_ok")
        ln_step = sem("ln_step")
        sdev_ok = sem("sdev_ok")
        cn_ok = sem("cn_ok")
        cT_ps = sem("cT_ps")
        cT_ok = sem("cT_ok")
        condT_ps = sem("condT_ps")
        condT_ok = sem("condT_ok")
        hid_ps = sem("hid_ps")
        hid_ok = sem("hid_ok")
        bup_ps = sem("bup_ps")
        bup_ok = sem("bup_ok")
        wmax_ok = sem("wmax_ok")
        wmax_all = sem("wmax_all")
        ws_step = sem("ws_step")
        whi_ok = sem("whi_ok")
        wlo_ok = sem("wlo_ok")
        bz_ok = sem("bz_ok")
        h0_zero = sem("h0_zero")
        h0_tr = sem("h0_tr")
        cond_l_ok = sem("cond_l_ok")
        h0_ps = sem("h0_ps")
        h0_ok = sem("h0_ok")

        with nc.Block() as block:
            @block.sync
            def _(sp):
                sp.dma_start(cond_sb, cond).then_inc(ld_cond, 16)
                sp.dma_start(gam, ln_gamma.partition_broadcast(NB)).then_inc(ld_small, 16)
                sp.dma_start(bet, ln_beta.partition_broadcast(NB)).then_inc(ld_small, 16)
                sp.dma_start(w1_sb, W1.rearrange("(c p) n -> p c n", p=P)).then_inc(ld_w1, 16)
                sp.dma_start(bup, base_up.rearrange("(c p) n -> p c n", p=P)).then_inc(ld_bup, 16)
                for q, rows in enumerate(lanes(Wh)):
                    sp.dma_start(wh32[32 * q:32 * q + 32], rows).then_inc(ld_wh, 16)
                for q, rows in enumerate(lanes(Wx)):
                    sp.dma_start(wx32[32 * q:32 * q + 32], rows).then_inc(ld_wx, 16)
                for q, rows in enumerate(lanes(base_down)):
                    sp.dma_start(based[32 * q:32 * q + 32], rows).then_inc(ld_based, 16)
                sp.wait_ge(ld_wx, 16 * KC)
                sp.wait_ge(ld_based, 16 * KC)

            @block.gpsimd
            def _(pool):
                nc.gpsimd.memset(ident[:], 0.0).then_inc(ident_zero, 1)
                pool.wait_ge(ident_zero, 1)
                nc.gpsimd.affine_select(out=ident[:], in_=ident[:], compare_op=ALU.not_equal, fill=1.0,
                                        base=0, pattern=[[-1, P]], channel_multiplier=1).then_inc(ident_ok, 1)
                nc.gpsimd.memset(own[:], 1.0).then_inc(own_step, 1)
                pool.wait_ge(own_step, 1)
                nc.gpsimd.affine_select(out=own[:], in_=own[:], compare_op=ALU.is_ge, fill=0.0, base=0,
                                        pattern=[[-R, NB], [0, TB]], channel_multiplier=1).then_inc(own_step, 1)
                pool.wait_ge(own_step, 2)
                nc.gpsimd.affine_select(out=own[:], in_=own[:], compare_op=ALU.is_ge, fill=0.0, base=R - 1,
                                        pattern=[[R, NB], [0, TB]], channel_multiplier=-1).then_inc(own_step, 1)
                with nc.allow_non_contiguous_dma("512 bias values, once"):
                    pool.dma_start(b1_sb, bias1.rearrange("(c p) -> p c", p=P)).then_inc(ld_bias, 16)
                bv = b.rearrange("(g q h c p) -> h c g q p", g=G, q=KC, h=2, c=2)
                for h in range(2):
                    for c in range(2):
                        pool.dma_start(brow[8 * h + c:8 * h + c + 7:2, :].rearrange("g (q p) -> g q p", q=KC),
                                       bv[h, c]).then_inc(ld_bias, 16)
                pool.wait_ge(wmax_ok, 5)
                nc.gpsimd.partition_all_reduce(wexp, winv, P, RMAX).then_inc(wmax_all, 1)

            @block.vector
            def _(dve):
                nc.vector.memset(banks[2][:], 0.0)
                nc.vector.memset(banks[3][:], 0.0).then_inc(h0_zero, 1)
                dve.wait_ge(ld_cond, 16)
                nc.vector.tensor_copy(lane_view(cond_l), in_lanes(cond_sb)).then_inc(cond_l_ok, 1)
                nc.vector.bn_stats(stats, cond_sb).then_inc(ln_step, 1)
                dve.wait_ge(ln_step, 1)
                nc.vector.bn_aggr(mv, stats).then_inc(ln_step, 1)
                dve.wait_ge(ln_step, 2)
                nc.vector.tensor_scalar(veps, mv[:, 1:2], LN_EPS, None, ALU.add).then_inc(ln_step, 1)
                dve.wait_ge(sdev_ok, 1)
                nc.vector.reciprocal(rstd, sdev).then_inc(ln_step, 1)
                dve.wait_ge(ln_step, 4)
                nc.vector.tensor_scalar(newt[:, 0:1], rstd, rstd, veps, ALU.mult, ALU.mult).then_inc(ln_step, 1)
                dve.wait_ge(ln_step, 5)
                nc.vector.tensor_scalar(newt[:, 1:2], newt[:, 0:1], -0.5, 1.5, ALU.mult, ALU.add).then_inc(ln_step, 1)
                dve.wait_ge(ln_step, 6)
                nc.vector.tensor_scalar(rstd, rstd, newt[:, 1:2], None, ALU.mult).then_inc(ln_step, 1)
                dve.wait_ge(ln_step, 7)
                nc.vector.tensor_scalar(cn, cond_sb, mv[:, 0:1], rstd, ALU.subtract, ALU.mult).then_inc(ln_step, 1)
                dve.wait_ge(ln_step, 8)
                dve.wait_ge(ld_small, 16 * 2)
                nc.vector.tensor_tensor(cn, cn, gam, ALU.mult).then_inc(ln_step, 1)
                dve.wait_ge(ln_step, 9)
                nc.vector.tensor_tensor(cn, cn, bet, ALU.add).then_inc(cn_ok, 1)
                dve.wait_ge(condT_ps, 1)
                nc.vector.tensor_copy(condT, banks[1][:, 0:KC * NB].rearrange("p (c n) -> p c n", c=KC)).then_inc(condT_ok, 1)
                dve.wait_ge(cT_ps, 1)
                nc.vector.tensor_copy(cT, banks[0][:, 0:KC * NB].rearrange("p (c n) -> p c n", c=KC)).then_inc(cT_ok, 1)
                for lc in range(KC):
                    dve.wait_ge(bup_ps, lc + 1)
                    nc.vector.tensor_scalar(lane_view(baseu[:, lc, :]), in_lanes(banks[4 + lc][:]), H_SCALE, None,
                                            ALU.mult).then_inc(bup_ok, 1)
                dve.wait_ge(ld_wh, 16 * KC)
                for kb in range(KC):
                    nc.vector.tensor_reduce(wmax[:, kb:kb + 1], wh32[:, kb, :], AX_X, ALU.max,
                                            apply_absolute_value=True).then_inc(wmax_ok, 1)
                dve.wait_ge(wmax_ok, 4)
                nc.vector.tensor_reduce(winv, wmax, AX_X, ALU.max).then_inc(wmax_ok, 1)
                dve.wait_ge(wmax_all, 1)
                nc.vector.tensor_scalar(wexp, wexp, MAX_FLOOR, None, ALU.max).then_inc(ws_step, 1)
                dve.wait_ge(ws_step, 1)
                nc.vector.tensor_scalar(wexp.bitcast(U32), wexp.bitcast(U32), EXPONENT_BITS, None,
                                        ALU.bitwise_and).then_inc(ws_step, 1)
                dve.wait_ge(ws_step, 2)
                nc.vector.reciprocal(winv, wexp).then_inc(ws_step, 1)
                dve.wait_ge(ws_step, 3)
                nc.vector.tensor_scalar(w_scale[:], winv, W_TOP, None, ALU.mult).then_inc(ws_step, 1)
                nc.vector.tensor_scalar(w_scale_h[:], winv, 0.5 * W_TOP, None, ALU.mult).then_inc(ws_step, 1)
                nc.vector.tensor_scalar(z_units[:], winv, W_TOP * H_SCALE, None, ALU.mult).then_inc(ws_step, 1)
                nc.vector.tensor_scalar(gate_scale[:], wexp, 1.0 / (W_TOP * H_SCALE), None, ALU.mult).then_inc(ws_step, 1)
                dve.wait_ge(ws_step, 7)
                for kb in range(KC):
                    for lo, hi, sc in ((0, 3 * D, w_scale_h), (3 * D, 4 * D, w_scale)):
                        nc.vector.tensor_scalar(wh_hi[:, kb, lo:hi], wh32[:, kb, lo:hi], sc[:, 0:1], None,
                                                ALU.mult).then_inc(whi_ok, 1)
                for kb in range(KC):
                    dve.wait_ge(whi_ok, 2 * kb + 2)
                    for lo, hi, sc in ((0, 3 * D, w_scale_h), (3 * D, 4 * D, w_scale)):
                        nc.vector.scalar_tensor_tensor(out=wh_lo[:, kb, lo:hi], in0=wh32[:, kb, lo:hi], scalar=sc[:, 0:1],
                                                       in1=wh_hi[:, kb, lo:hi], op0=ALU.mult,
                                                       op1=ALU.subtract).then_inc(wlo_ok, 1)
                nc.vector.tensor_scalar(bias_z[:], banks[1][:, 64:64 + NCB], z_units[:, 0:1], None,
                                        ALU.mult).then_inc(bz_ok, 1)
                dve.wait_ge(bz_ok, 1)
                for half in range(2):
                    nc.vector.tensor_scalar(bias_z[:, 8 * half:8 * half + 6], bias_z[:, 8 * half:8 * half + 6], 0.5, None,
                                            ALU.mult).then_inc(bz_ok, 1)
                dve.wait_ge(h0_ps, 1)
                for half in range(2):
                    nc.vector.transpose(h0_t[:, half].rearrange("p a b -> p (a b)"), banks[2 + half][:, 0:256]).then_inc(h0_tr, 1)
                dve.wait_ge(h0_tr, 2)
                for half in range(2):
                    nc.vector.tensor_scalar(h0_z[:, 8 * half:8 * half + 6, :], h0_t[:, half, 0:6, 0:NB], z_units[:, 0:1], 0.5,
                                            ALU.mult, ALU.mult).then_inc(h0_ok, 1)
                    nc.vector.tensor_scalar(h0_z[:, 8 * half + 6:8 * half + 8, :], h0_t[:, half, 6:8, 0:NB],
                                            z_units[:, 0:1], None, ALU.mult).then_inc(h0_ok, 1)

            @block.scalar
            def _(act):
                act.wait_ge(ln_step, 3)
                nc.scalar.activation(sdev, veps, ACT.Sqrt).then_inc(sdev_ok, 1)
                act.wait_ge(ld_bias, 16 * 5)
                for i in range(KC):
                    act.wait_ge(hid_ps, i + 1)
                    nc.scalar.activation(hidT[:, i, :], banks[0][:, 64 + i * NB:64 + (i + 1) * NB], ACT.Gelu,
                                         bias=b1_sb[:, i:i + 1]).then_inc(hid_ok, 1)
                act.wait_ge(ld_wx, 16 * KC)
                for kb in range(KC):
                    for g in range(G):
                        for half in range(2):
                            cb = 8 * half + 2 * g
                            src = wx32[:, kb, g * D:(g + 1) * D].rearrange("p (q h c l) -> p h c q l", q=KC, h=2, c=2)
                            nc.scalar.activation(wx_l[:, kb, cb:cb + 2, :].rearrange("p c (q l) -> p c q l", q=KC),
                                                 src[:, half], ACT.Copy, scale=0.5 if g < 3 else 1.0).then_inc(wx_ok, 1)

            @block.tensor
            def _(pe):
                pe.wait_ge(ident_ok, 1)
                pe.wait_ge(cond_l_ok, 1)
                for B in range(KC):
                    mm = nc.tensor.transpose(banks[1][:, B * NB:(B + 1) * NB], cond_l[:, B * P:(B + 1) * P], ident[0:NB, 0:NB])
                pe.wait_ge(ld_bias, 16 * 5)
                nc.tensor.transpose(banks[1][:, 64:64 + NCB], brow, ident[0:NCB, 0:NCB]).then_inc(condT_ps, 1)
                pe.wait_ge(ld_bup, 16)
                for lc in range(KC):
                    for kc in range(KC):
                        mm = nc.tensor.transpose(banks[4 + lc][:, kc * P:(kc + 1) * P], bup[:, kc, lc * P:(lc + 1) * P],
                                                 ident[:])
                    mm.then_inc(bup_ps, 1)
                pe.wait_ge(cn_ok, 1)
                for c in range(KC):
                    mm = nc.tensor.transpose(banks[0][:, c * NB:(c + 1) * NB], cn[:, c * P:(c + 1) * P], ident[0:NB, 0:NB])
                mm.then_inc(cT_ps, 1)
                pe.wait_ge(cT_ok, 1)
                pe.wait_ge(ld_w1, 16)
                for i in range(KC):
                    if i:
                        pe.wait_ge(hid_ok, i)
                    for c in range(KC):
                        mm = nc.tensor.matmul(banks[0][:, 64 + i * NB:64 + (i + 1) * NB], w1_sb[:, c, i * P:(i + 1) * P], cT[:, c, :],
                                              start=(c == 0), stop=(c == KC - 1))
                    mm.then_inc(hid_ps, 1)
                pe.wait_ge(condT_ok, 1)
                pe.wait_ge(ld_wh, 16 * KC)
                pe.wait_ge(h0_zero, 1)
                for half in range(2):
                    for kb in range(KC):
                        for q in range(KC):
                            mm = nc.tensor.matmul(
                                banks[2 + half][32 * q:32 * q + NB, 0:256], condT[:, kb, :],
                                wh32[:, kb, :].rearrange("p (g q c) -> p g q c", g=G, q=KC)[:, :, q, 64 * half:64 * half + 64],
                                start=(kb == 0), stop=(kb == KC - 1), tile_position=(0, 32 * q))
                mm.then_inc(h0_ps, 1)

        at[0] = 0
        NW = 4
        w2_sb = [take(P, KC, 512) for _ in range(NW)]
        b2_sb = [take(NB, 512) for _ in range(NW)]
        ad_sb = [take(NB, R, DBL) for _ in range(NW)]
        ld_w2 = [sem(f"ld_w2_{i}") for i in range(NW)]
        ad_ps = sem("ad_ps")
        ad_ok = sem("ad_ok")
        st_ad = [sem(f"st_ad_{i}") for i in range(NW)]
        w2_v = W2.rearrange("(c p) (w n) -> w p c n", p=P, n=512)
        bias2_v = bias2.rearrange("(w n) -> w n", n=512)

        with nc.Block() as block:
            @block.sync
            def _(sp):
                for i in range(NW):
                    sp.dma_start(w2_sb[i], w2_v[i]).then_inc(ld_w2[i], 16)
                    sp.dma_start(b2_sb[i], bias2_v[i].partition_broadcast(NB)).then_inc(ld_w2[i], 16)
                with sp.Fori(1, WCH // NW) as r:
                    for i in range(NW):
                        sp.wait_ge(ad_ok, (r - 1) * NW + (i + 1))
                        sp.sem_inc(pace["sp"], 1)
                        sp.dma_start(w2_sb[i], w2_v[bass.ds(r * NW + i, 1)].rearrange("a p c n -> p (a c) n")).then_inc(ld_w2[i], 16)
                        sp.dma_start(b2_sb[i], bias2_v[bass.ds(r * NW + i, 1), :].rearrange("a n -> (a n)").partition_broadcast(NB)
                                     ).then_inc(ld_w2[i], 16)

            @block.tensor
            def _(pe):
                def turn(r, first):
                    for i in range(NW):
                        pe.wait_ge(ld_w2[i], r * 32 + 32)
                        if i == 0 and not first:
                            pe.wait_ge(ad_ok, r * NW)
                        for c in range(KC):
                            mm = nc.tensor.matmul(banks[i][0:NB, :], hidT[:, c, :], w2_sb[i][:, c, :],
                                                  start=(c == 0), stop=(c == KC - 1))
                        mm.then_inc(ad_ps, 1)

                turn(0, True)
                with pe.Fori(1, WCH // NW) as r:
                    turn(r, False)

            @block.vector
            def _(dve):
                def turn(r, first):
                    for i in range(NW):
                        dve.wait_ge(ad_ps, r * NW + (i + 1))
                        if not first:
                            dve.wait_ge(st_ad[i], r * 16)
                        nc.vector.tensor_tensor(ad_sb[i].rearrange("b r d -> b d r"),
                                                banks[i][0:NB, :].rearrange("b (d r) -> b d r", r=R),
                                                b2_sb[i].rearrange("b (d r) -> b d r", r=R), ALU.add).then_inc(ad_ok, 1)

                turn(0, True)
                with dve.Fori(1, WCH // NW) as r:
                    turn(r, False)

            @block.scalar
            def _(act):
                with act.Fori(0, WCH // NW) as r:
                    for i in range(NW):
                        act.wait_ge(ad_ok, r * NW + (i + 1))
                        act.dma_start(adapt_dram[bass.ds(r * NW + i, 1)].rearrange("a b r d -> (a b) r d"),
                                      ad_sb[i]).then_inc(st_ad[i], 16)
                for i in range(NW):
                    act.wait_ge(st_ad[i], 16 * WCH // NW)

        at[0] = 0
        a2_t = take(BR, D)
        b1_t = take(BR, D)
        a1_raw = take(BR, D)
        ld_nat = sem("ld_nat")
        ld_lane = sem("ld_lane")
        fac_ps = sem("fac_ps")
        fac_ok = sem("fac_ok")
        a1_ok = sem("a1_ok")

        with nc.Block() as block:
            @block.sync
            def _(sp):
                ad_v = adapt_dram.rearrange("(j q h) b r (c p) -> j h c (b r) q p", j=4, q=KC, c=2)
                for j, dst in ((1, b1_t), (3, b2_t[:])):
                    sp.dma_start(dst.rearrange("r (w d) -> r w d", d=DBL),
                                 adapt_dram[8 * j:8 * j + 8].rearrange("w b r d -> (b r) w d")).then_inc(ld_nat, 16)
                for j, dst in ((2, a2_t), (0, a1_raw)):
                    for B in range(KC):
                        sp.dma_start(dst[:, B * P:(B + 1) * P].rearrange("r (q p) -> r q p", q=KC),
                                     ad_v[j, B // 2, B % 2]).then_inc(ld_lane, 16)
                sp.wait_ge(ld_nat, 32)
                sp.wait_ge(ld_lane, 16 * 2 * KC)

            @block.tensor
            def _(pe):
                pe.wait_ge(ld_nat, 32)
                pe.wait_ge(ld_lane, 16 * 2 * KC)
                for k in range(KC):
                    mm = nc.tensor.transpose(banks[0][:, k * BR:(k + 1) * BR], a2_t[:, k * P:(k + 1) * P], ident[0:BR, 0:BR])
                mm.then_inc(fac_ps, 1)
                for k in range(KC):
                    mm = nc.tensor.transpose(banks[1][:, k * BR:(k + 1) * BR], b1_t[:, k * P:(k + 1) * P], ident[0:BR, 0:BR])
                mm.then_inc(fac_ps, 1)

            @block.vector
            def _(dve):
                for i, dst in enumerate((a2_c, b1_c)):
                    dve.wait_ge(fac_ps, i + 1)
                    nc.vector.tensor_copy(dst[:], banks[i][:, 0:KC * BR].rearrange("p (k r) -> p k r", k=KC)).then_inc(fac_ok, 1)
                dve.wait_ge(ld_lane, 16 * 2 * KC)
                nc.vector.tensor_scalar(a1_t[:], a1_raw, H_SCALE, None, ALU.mult).then_inc(a1_ok, 1)

        at[0] = 0
        XS = 4
        xz = take(P, NCB, NB, 2 * TB)
        x2s = take(P, XS * KC, TOK)
        hs = take(P, KC, NB, 2 * TB)
        xn = take(P, TT, D)
        xl = take(P, TT, D)
        xT = take(P, KC, TOK)
        midT = take(P, KC, TOK)
        um = take(BR, NB, TB)
        vm = take(BR, NB, TB)
        y_t = take(P, P)
        y_n = [take(P, D) for _ in range(TT)]
        h_st = sb("h_st", [P, 2, KC, 2 * NB], F16)
        zt = [sb(f"zt{i}", [P, 8, 32], F32) for i in range(2)]
        u = [sb(f"u{i}", [P, 8, NB], F32) for i in range(2)]
        z = [sb(f"z{i}", [P, 8, NB], F32) for i in range(2)]
        gt = [sb(f"gt{i}", [P, 10, NB], F32) for i in range(2)]
        os_ = [sb(f"os{i}", [P, 2, NB], F32) for i in range(2)]
        parts = [sb(f"parts{i}", [P, 4, NB], F32) for i in range(2)]
        cell2 = [g[:, 8:10, :] for g in gt]
        xc = sb("xc", [P, NCB, NB], F32)
        hc = sb("hc", [P, 2, KC, NB], F32)
        tc = [sb(f"tc{i}", [P, 2, NB], F32) for i in range(2)]

        def pair(name):
            return [sem(f"{name}0"), sem(f"{name}1")]

        state_ok = sem("state_ok")
        z_ps = pair("z_ps")
        zt_ok = pair("zt_ok")
        u_ok = pair("u_ok")
        z_ok = pair("z_ok")
        gt_ok = pair("gt_ok")
        parts_ok = pair("parts_ok")
        xc_ok = sem("xc_ok")
        hs_ok = sem("hs_ok")
        cell_ok = pair("cell_ok")
        tc_ok = pair("tc_ok")
        h32_ok = pair("h32_ok")
        h_ok = pair("h_ok")
        proj_ps = sem("proj_ps")
        proj_ok = sem("proj_ok")
        h0_in = sem("h0_in")
        ld_xn = sem("ld_xn")
        xl_ok = sem("xl_ok")
        xT_ps = sem("xT_ps")
        xT_ok = sem("xT_ok")
        um_ps = sem("um_ps")
        um_ok = sem("um_ok")
        mid_ps = sem("mid_ps")
        mid_ok = sem("mid_ok")
        vm_ps = sem("vm_ps")
        vm_ok = sem("vm_ok")
        out_ps = sem("out_ps")
        x2_ok = sem("x2_ok")
        y_add = sem("y_add")
        y_ps = sem("y_ps")
        y_ok = sem("y_ok")
        y_free = pair("y_free")
        st_y = sem("st_y")

        z_bank = banks[0:2]
        proj_bank = banks[2:4]
        mix_bank = banks[4:7]
        y_bank = banks[7]
        wh_v = [w[:].rearrange("p k (g q c) -> p k g q c", g=G, q=KC) for w in (wh_hi, wh_lo)]
        x_v = x.rearrange("b (m t) d -> m b t d", t=TB)
        out_v = out.rearrange("b (m t) d -> m b t d", t=TB)
        x2s_t = x2s.rearrange("p c (b t) -> p (c b) t", t=TB)
        hs_t = hs.rearrange("p c b t -> p (c b) t")

        def mix_out(i):
            return mix_bank[i % 3]

        MID_AT, OUT_AT, MIX_END = 7, 20, 30
        TERMS = KC + 1

        def last_step(base, k):
            return base + (TERMS * k + TERMS - 1) // 2

        with nc.Block() as block:
            @block.sync
            def _(sp):
                def load_x(m):
                    for bt in range(NB):
                        sp.dma_start(xn[TB * (bt % BPT):TB * (bt % BPT + 1), bt // BPT, :],
                                     x_v[bass.ds(m & (NBLK - 1), 1), bt].rearrange("m t d -> (m t) d")).then_inc(ld_xn, 16)

                def store_y(n, tt):
                    sp.wait_ge(y_ok, n * (TT * KC) + (tt * KC + KC + 1))
                    sp.sem_inc(pace["sp"], 1)
                    for i in range(BPT):
                        sp.dma_start(out_v[bass.ds((n + NBLK - 1) & (NBLK - 1), 1), tt * BPT + i].rearrange(
                            "m t d -> (m t) d"), y_n[tt][TB * i:TB * (i + 1), :]).then_inc(st_y, 16)
                    sp.wait_ge(st_y, n * (16 * NB) + 16 * BPT * (tt + 1))
                    sp.sem_inc(y_free[tt], 1)

                load_x(0)
                for m in range(1, 4):
                    sp.wait_ge(xl_ok, TT * m)
                    load_x(m)
                for tt in range(TT):
                    sp.sem_inc(y_free[tt], 1)
                with sp.Fori(0, NBLK) as n:
                    store_y(n, 0)
                    sp.wait_ge(xl_ok, n * TT + TT * 4)
                    sp.sem_inc(pace["sp"], 1)
                    load_x(n + 4)
                    store_y(n, 1)
                for tt in range(TT):
                    store_y(NBLK, tt)
                sp.wait_ge(ld_xn, 16 * NB * (NBLK + 4))
                sp.wait_ge(st_y, 16 * NB * (NBLK + 1))

            @block.gpsimd
            def _(pool):
                def x_lane(m, tt):
                    if tt == 0:
                        pool.wait_ge(ld_xn, m * (16 * NB) + 16 * NB)
                        if not isinstance(m, int) or m > 0:
                            pool.wait_ge(xT_ps, m * KC)
                        pool.sem_inc(pace["pool"], 1)
                    nc.gpsimd.tensor_copy(lane_view(xl[:, tt, :]), in_lanes(xn[:, tt, :])).then_inc(xl_ok, 1)

                def y_sum(n, k):
                    tt, B = k // KC, k % KC
                    if k == 0:
                        pool.wait_ge(hs_ok, n * TB + 2)
                    pool.wait_ge(y_ps, n * (TT * KC) + (k + 1))
                    nc.gpsimd.tensor_tensor(
                        y_t.rearrange("p (b t) -> p b t", t=TB),
                        hs_t[:, B * NB + tt * BPT:B * NB + (tt + 1) * BPT, bass.ds(((n + 1) & 1) * TB, TB)],
                        x2s_t[:, bass.ds(((n + 3) & (XS - 1)) * (KC * NB) + (B * NB + tt * BPT), BPT), :],
                        ALU.add).then_inc(y_add, 1)

                def keep_h(s, pos, t):
                    pool.wait_ge(h32_ok[0], t + 1)
                    pool.wait_ge(h32_ok[1], t + 1)
                    pool.sem_inc(pace["pool"], 1)
                    nc.gpsimd.tensor_copy(hs[:, :, :, bass.ds(pos, 1)].rearrange("p c b t -> p c (b t)"),
                                          hc[:, s & 1]).then_inc(hs_ok, 1)

                for m in range(3):
                    for tt in range(TT):
                        x_lane(m, tt)
                pool.wait_ge(state_ok, 7)
                pool.sem_inc(hs_ok, 2)
                with pool.Fori(0, NBLK) as n:
                    for s in range(TB):
                        if s % KC == 0:
                            y_sum(n, s // KC)
                        if s % KC == 2 and s // KC in (1, 3):
                            x_lane(n + 3, s // (2 * KC))
                        keep_h(s, (n & 1) * TB + s, n * TB + s)
                for k in range(TT * KC):
                    y_sum(NBLK, k)

            @block.tensor
            def _(pe):
                def mix(m, s):
                    if s < KC:
                        B = s
                        if B == 0:
                            pe.wait_ge(xl_ok, m * TT + TT)
                        if B < 3:
                            if not isinstance(m, int) or m > 0:
                                pe.wait_ge(x2_ok, m * KC)
                        else:
                            pe.wait_ge(xT_ok, m * KC + 1)
                        for tt in range(TT):
                            mm = nc.tensor.transpose(mix_out(B)[:, tt * P:(tt + 1) * P],
                                                     xl[:, tt, B * P:(B + 1) * P], ident[:])
                        mm.then_inc(xT_ps, 1)
                    if s in (5, 6):
                        pe.wait_ge(xT_ok, m * KC + KC)
                        for B in (2 * (s - 5), 2 * (s - 5) + 1):
                            mm = nc.tensor.matmul(mix_out(4)[0:BR, 0:TOK], a2_c[:, B, :], xT[:, B, :],
                                                  start=(B == 0), stop=(B == KC - 1))
                        if s == 6:
                            mm.then_inc(um_ps, 1)
                    if MID_AT <= s < MID_AT + TERMS * KC // 2:
                        for i in (2 * (s - MID_AT), 2 * (s - MID_AT) + 1):
                            lc, term = i // TERMS, i % TERMS
                            if term == 0 and lc == 2:
                                pe.wait_ge(um_ok, m + 1)
                            if term == 0 and lc == 3:
                                pe.wait_ge(mid_ok, m * KC + 1)
                            if term < KC:
                                mm = nc.tensor.matmul(mix_out(5 + lc)[:, 0:TOK], based[:, term, lc * P:(lc + 1) * P],
                                                      xT[:, term, :], start=(term == 0), stop=False)
                            else:
                                if lc == 0:
                                    pe.wait_ge(um_ok, m + 1)
                                nc.tensor.matmul(mix_out(5 + lc)[:, 0:TOK], b2_t[:, lc * P:(lc + 1) * P],
                                                 um.rearrange("p b t -> p (b t)"), start=False,
                                                 stop=True).then_inc(mid_ps, 1)
                    if s in (18, 19):
                        pe.wait_ge(mid_ok, m * KC + KC)
                        for lc in (2 * (s - 18), 2 * (s - 18) + 1):
                            mm = nc.tensor.matmul(mix_out(9)[0:BR, 0:TOK], b1_c[:, lc, :], midT[:, lc, :],
                                                  start=(lc == 0), stop=(lc == KC - 1))
                        if s == 19:
                            mm.then_inc(vm_ps, 1)
                    if OUT_AT <= s < OUT_AT + TERMS * KC // 2:
                        for i in (2 * (s - OUT_AT), 2 * (s - OUT_AT) + 1):
                            B, term = i // TERMS, i % TERMS
                            if term == 0 and B == 2:
                                pe.wait_ge(vm_ok, m + 1)
                            if term == 0 and B == 3:
                                pe.wait_ge(x2_ok, m * KC + 1)
                            if term < KC:
                                mm = nc.tensor.matmul(mix_out(10 + B)[:, 0:TOK], baseu[:, term, B * P:(B + 1) * P],
                                                      midT[:, term, :], start=(term == 0), stop=False)
                            else:
                                if B == 0:
                                    pe.wait_ge(vm_ok, m + 1)
                                nc.tensor.matmul(mix_out(10 + B)[:, 0:TOK], a1_t[:, B * P:(B + 1) * P],
                                                 vm.rearrange("p b t -> p (b t)"), start=False,
                                                 stop=True).then_inc(out_ps, 1)

                def project(m, s):
                    turn, kb = s // KC, s % KC
                    if kb == 0 and (turn > 0 or not isinstance(m, int) or m > 0):
                        pe.wait_ge(proj_ok, m * NCB + 2 * turn)
                    if s == 0:
                        pe.wait_ge(x2_ok, m * KC + KC)
                    for i in range(2):
                        mm = nc.tensor.matmul(
                            proj_bank[i][:, 0:TOK], wx_l[:, kb, 2 * turn + i, :],
                            x2s[:, bass.ds((m & (XS - 1)) * KC + kb, 1), :].rearrange("p a t -> p (a t)"),
                            start=(kb == 0), stop=(kb == KC - 1))
                        if kb == KC - 1:
                            mm.then_inc(proj_ps, 1)

                def turn_y(n, k):
                    pe.wait_ge(y_add, n * (TT * KC) + (k + 1))
                    pe.wait_ge(y_ok, n * (TT * KC) + (k + 1))
                    nc.tensor.transpose(y_bank[:, 0:P], y_t, ident[:]).then_inc(y_ps, 1)

                def recur(parity, n_half, chunks, start=False, stop=False):
                    for kb in chunks:
                        for part in range(2):
                            for q in range(KC):
                                mm = nc.tensor.matmul(
                                    z_bank[n_half][32 * q:32 * q + 2 * NB, 0:256], h_st[:, parity, kb, :],
                                    wh_v[part][:, kb, :, q, 64 * n_half:64 * n_half + 64],
                                    start=(start and kb == chunks[0] and part == 0),
                                    stop=(stop and kb == chunks[-1] and part == 1), tile_position=(0, 32 * q))
                    return mm

                pe.sem_inc(y_ps, 1)
                for m in range(2):
                    for s in range(MIX_END):
                        mix(m, s)
                for s in range(TB):
                    project(0, s)
                pe.wait_ge(state_ok, 7)

                with pe.Fori(0, NBLK) as n:
                    for s in range(TB):
                        t = n * TB + s
                        par = s & 1
                        project(n + 1, s)
                        mix(n + 2, s)
                        if s % KC == 1:
                            turn_y(n, s // KC)
                        pe.wait_ge(h_ok[0], t + 1)
                        recur(par, 0, (0, 1), start=True)
                        recur(par, 1, (0,), start=True)
                        pe.wait_ge(h_ok[1], t + 1)
                        recur(par, 0, (2, 3), stop=True).then_inc(z_ps[0], 1)
                        recur(par, 1, (1,))
                        recur(par, 1, (2, 3), stop=True).then_inc(z_ps[1], 1)
                for k in range(TT * KC):
                    turn_y(NBLK, k)

            @block.scalar
            def _(act):
                gate_s = act.alloc_register("gate_s")
                proj_s = act.alloc_register("proj_s")
                act.reg_load(gate_s, gate_scale[0:1, 0:1].bitcast(U32))
                act.reg_load(proj_s, w_scale[0:1, 0:1].bitcast(U32))

                def mix(m, s):
                    if s < KC:
                        act.wait_ge(xT_ps, m * KC + (s + 1))
                        nc.scalar.activation(xT[:, s, :], mix_out(s)[:, 0:TOK], ACT.Copy).then_inc(xT_ok, 1)
                    for lc in range(KC):
                        if s == last_step(MID_AT, lc):
                            act.wait_ge(mid_ps, m * KC + (lc + 1))
                            nc.scalar.activation(midT[:, lc, :], mix_out(5 + lc)[:, 0:TOK], ACT.Gelu).then_inc(mid_ok, 1)

                def take_projection(m, turn):
                    for i in range(2):
                        cb = 2 * turn + i
                        act.wait_ge(proj_ps, m * NCB + (cb + 1))
                        nc.scalar.activation(xz[:, cb, :, bass.ds((m & 1) * TB, TB)],
                                             proj_bank[i][:, 0:TOK].rearrange("p (b t) -> p b t", t=TB), ACT.Identity,
                                             bias=bias_z[:, cb:cb + 1], scale=proj_s).then_inc(proj_ok, 1)

                def xz_step(pos):
                    nc.scalar.activation(xc[:], xz[:, :, :, bass.ds(pos, 1)].rearrange("p a b t -> p a (b t)"),
                                         ACT.Copy).then_inc(xc_ok, 1)

                def take_y(n, k):
                    tt, B = k // KC, k % KC
                    act.wait_ge(y_ps, n * (TT * KC) + (k + 2))
                    if B == 0:
                        act.wait_ge(y_free[tt], n + 1)
                    nc.scalar.activation(y_n[tt].rearrange("a (q B p) -> a B q p", q=KC, B=KC)[:, B],
                                         y_bank[:, 0:P].rearrange("a (q p) -> a q p", q=KC), ACT.Copy,
                                         scale=1.0 / H_SCALE).then_inc(y_ok, 1)

                act.sem_inc(y_ok, 1)
                for m in range(2):
                    for s in range(MIX_END):
                        mix(m, s)
                for turn in range(TB // KC):
                    take_projection(0, turn)

                with act.Fori(0, NBLK) as n:
                    for s in range(TB):
                        t = n * TB + s
                        if s > 0:
                            xz_step((n & 1) * TB + s)
                        else:
                            act.wait_ge(h0_in, 1)
                            xz_step((n & 1) * TB)
                        mix(n + 2, s)
                        if s % KC == KC - 1:
                            take_projection(n + 1, s // KC)
                        if s % KC == 1:
                            take_y(n, s // KC)
                        for half in range(2):
                            act.wait_ge(z_ok[half], t + 1)
                            nc.scalar.activation(gt[half][:, 0:8, :], z[half][:], ACT.Tanh, scale=gate_s).then_inc(gt_ok[half], 1)
                            act.wait_ge(gt_ok[half], t + 1)
                            nc.scalar.activation(os_[half][:], gt[half][:, 4:6, :], ACT.Copy, bias=0.5 * H_SCALE,
                                                 scale=0.5 * H_SCALE)
                            act.wait_ge(cell_ok[half], t + 1)
                            nc.scalar.activation(tc[half][:], cell2[half], ACT.Tanh, scale=0.5).then_inc(tc_ok[half], 1)
                for k in range(TT * KC):
                    take_y(NBLK, k)

            @block.vector
            def _(dve):
                def mix(m, s):
                    if s == 6:
                        dve.wait_ge(um_ps, m + 1)
                        nc.vector.tensor_tensor(um, mix_out(4)[0:BR, 0:TOK].rearrange("p (b t) -> p b t", t=TB), own[:],
                                                ALU.mult).then_inc(um_ok, 1)
                    if s == 19:
                        dve.wait_ge(vm_ps, m + 1)
                        nc.vector.tensor_tensor(vm, mix_out(9)[0:BR, 0:TOK].rearrange("p (b t) -> p b t", t=TB), own[:],
                                                ALU.mult).then_inc(vm_ok, 1)
                    for B in range(KC):
                        if s == last_step(OUT_AT, B):
                            dve.wait_ge(out_ps, m * KC + (B + 1))
                            nc.vector.scalar_tensor_tensor(
                                out=x2s[:, bass.ds((m & (XS - 1)) * KC + B, 1), :].rearrange("p a t -> p (a t)"),
                                in0=xT[:, B, :], scalar=2.0 * H_SCALE, in1=mix_out(10 + B)[:, 0:TOK], op0=ALU.mult,
                                op1=ALU.add).then_inc(x2_ok, 1)

                def to_lanes(half, t):
                    dve.wait_ge(z_ps[half], t + 1)
                    nc.vector.transpose(zt[half][:].rearrange("p a b -> p (a b)"),
                                        z_bank[half][:, 0:256]).then_inc(zt_ok[half], 1)

                def add_projection(half, t):
                    dve.wait_ge(zt_ok[half], t + 1)
                    nc.vector.tensor_tensor(u[half][:], zt[half][:, :, 0:NB],
                                            xc[:, 8 * half:8 * half + 8, :], ALU.add).then_inc(u_ok[half], 1)

                def add_low(half, t):
                    dve.wait_ge(u_ok[half], t + 1)
                    nc.vector.tensor_tensor(z[half][:], zt[half][:, :, NB:2 * NB], u[half][:],
                                            ALU.add).then_inc(z_ok[half], 1)

                def cell_parts(half, t):
                    dve.wait_ge(gt_ok[half], t + 1)
                    nc.vector.scalar_tensor_tensor(out=parts[half][:], in0=gt[half][:, 0:4, :], scalar=1.0,
                                                   in1=gt[half][:, 6:10, :], op0=ALU.add,
                                                   op1=ALU.mult).then_inc(parts_ok[half], 1)

                def new_cell(half, t):
                    dve.wait_ge(parts_ok[half], t + 1)
                    nc.vector.scalar_tensor_tensor(out=cell2[half], in0=parts[half][:, 2:4, :], scalar=0.5,
                                                   in1=parts[half][:, 0:2, :], op0=ALU.mult,
                                                   op1=ALU.add).then_inc(cell_ok[half], 1)

                def new_h(half, par, t):
                    ch = slice(2 * half, 2 * half + 2)
                    dve.wait_ge(tc_ok[half], t + 1)
                    nc.vector.tensor_tensor(h_st[:, 1 - par, ch, 0:NB], os_[half][:], tc[half][:], ALU.mult)
                    nc.vector.tensor_tensor(hc[:, par, ch, :], os_[half][:], tc[half][:],
                                            ALU.mult).then_inc(h32_ok[half], 1)

                def h_rest(half, par, t):
                    ch = slice(2 * half, 2 * half + 2)
                    dve.wait_ge(h32_ok[half], t + 1)
                    nc.vector.tensor_tensor(h_st[:, 1 - par, ch, NB:2 * NB], hc[:, par, ch, :],
                                            h_st[:, 1 - par, ch, 0:NB], ALU.subtract).then_inc(h_ok[half], 1)

                nc.vector.memset(h_st[:], 0.0).then_inc(state_ok, 1)
                for half in range(2):
                    nc.vector.memset(z_bank[half][:], 0.0).then_inc(state_ok, 1)
                nc.vector.memset(x2s[:, (XS - 1) * KC:XS * KC, :], 0.0).then_inc(state_ok, 1)
                nc.vector.memset(hs, 0.0).then_inc(state_ok, 1)
                for half in range(2):
                    nc.vector.memset(cell2[half], 0.0).then_inc(state_ok, 1)
                dve.wait_ge(state_ok, 7)
                for half in range(2):
                    dve.sem_inc(h_ok[half], 1)
                for m in range(2):
                    for s in range(MIX_END):
                        mix(m, s)
                dve.wait_ge(proj_ok, NCB)
                nc.vector.tensor_tensor(xz[:, :, :, 0], xz[:, :, :, 0], h0_z[:], ALU.add).then_inc(h0_in, 1)

                with dve.Fori(0, NBLK) as n:
                    for s in range(TB):
                        t = n * TB + s
                        par = s & 1
                        mix(n + 2, s)
                        dve.wait_ge(xc_ok, t + 1)
                        dve.wait_ge(hs_ok, t + 1)
                        to_lanes(0, t)
                        add_projection(0, t)
                        add_low(0, t)
                        to_lanes(1, t)
                        cell_parts(0, t)
                        add_projection(1, t)
                        new_cell(0, t)
                        add_low(1, t)
                        new_h(0, par, t)
                        h_rest(0, par, t)
                        cell_parts(1, t)
                        new_cell(1, t)
                        new_h(1, par, t)
                        h_rest(1, par, t)


_INS = ['x', 'cond_1024', 'L0_cond_base_up', 'L0_cond_base_down', 'L0_cond_ln_gamma', 'L0_cond_ln_beta',
        'L0_cond_W1', 'L0_cond_bias1', 'L0_cond_W2', 'L0_cond_bias2', 'L1_cond_Wx', 'L1_cond_Wh', 'L1_cond_b']
_OUTS = [((8, 1024, 512), 'float32')]


def kernel(**inputs):
    import numpy as _np
    import concourse.bacc as _bacc
    from concourse import mybir as _mybir
    from concourse.bass_utils import run_bass_kernel_spmd as _run

    nc = _bacc.Bacc("TRN2", target_bir_lowering=False, num_devices=1)
    arrays, args = {}, []
    for name in _INS:
        a = _np.ascontiguousarray(inputs[name])
        arrays[f"in_{name}_dram"] = a
        args.append(nc.dram_tensor(f"in_{name}_dram", a.shape, _mybir.dt.from_np(a.dtype), kind="ExternalInput").ap())
    for i, (shape, dtype) in enumerate(_OUTS):
        dt = _mybir.dt.from_np(_np.dtype(dtype))
        args.append(nc.dram_tensor(f"out_{i}_dram", shape, dt, kind="ExternalOutput").ap())
    lowrank_mixer_then_lstm(nc, *args)
    r = _run(nc, [arrays], core_ids=[0])
    got = tuple(r.results[0][f"out_{i}_dram"] for i in range(len(_OUTS)))
    return got[0]
```

```python
from contextlib import ExitStack

import concourse.bass as bass
from concourse import mybir

ALU = mybir.AluOpType
ACT = mybir.ActivationFunctionType
F32 = mybir.dt.float32
F16 = mybir.dt.float16
U32 = mybir.dt.uint32
AX_X = mybir.AxisListType.X
RMAX = bass.bass_isa.ReduceOp.max

P = 128
LN_EPS = 1e-5

H_SCALE = 2.0 ** 15
W_TOP = 2.0 ** 14
MAX_FLOOR = 2.0 ** -40
EXPONENT_BITS = 0x7F800000


def lowrank_mixer_then_lstm(nc, x, cond, base_up, base_down, ln_gamma, ln_beta, W1, bias1,
                            W2, bias2, Wx, Wh, b, out):
    NB, T, D = x.shape
    KC = D // P
    G = Wh.shape[1] // D
    R = W2.shape[1] // D // 4
    NG4 = G * D
    TB = 32
    NBLK = T // TB
    NCB = G * KC
    TOK = NB * TB
    TT = TOK // P
    BPT = NB // TT
    WT = 4 * KC
    BR = NB * R
    assert (NB, KC, G, R, NCB, TT) == (8, 4, 4, 8, 16, 2) and D == 512

    def lanes(w):
        return [w[P * q:P * (q + 1), :].rearrange("(B p) n -> p B n", p=32) for q in range(KC)]

    def in_lanes(ap):
        return ap.rearrange("a (q B p) -> a q B p", q=KC, B=KC)

    def lane_view(ap):
        return ap.rearrange("a (B q p) -> a q B p", q=KC, B=KC)

    with ExitStack() as ctx:
        def sb(name, shape, dt):
            return ctx.enter_context(nc.sbuf_tensor(name, shape, dt))

        def sem(name):
            return ctx.enter_context(nc.semaphore(name))

        banks = [ctx.enter_context(nc.psum_tensor(f"bank{i}", [P, 512], F32)) for i in range(8)]

        pace = {e: sem(f"pace_{e}") for e in ("sp", "pool", "dve")}

        ident = sb("ident", [P, P], F32)
        wh_hi = sb("wh_hi", [P, KC, NG4], F16)
        wh_lo = sb("wh_lo", [P, KC, NG4], F16)
        wx_l = sb("wx_l", [P, KC, NCB, P], F32)
        based = sb("based", [P, KC, D], F32)
        baseu = sb("baseu", [P, KC, D], F32)
        a2_c = sb("a2_c", [P, KC, BR], F32)
        b1_c = sb("b1_c", [P, KC, BR], F32)
        b2_t = sb("b2_t", [2 * BR, D], F32)
        a1_t = sb("a1_t", [2 * BR, D], F32)
        own = sb("own", [2 * BR, NB, TB], F32)
        bias_z = sb("bias_z", [P, NCB], F32)
        h0_z = sb("h0_z", [P, NCB, NB], F32)
        w_scale = sb("w_scale", [P, 1], F32)
        w_scale_h = sb("w_scale_h", [P, 1], F32)
        gate_scale = sb("gate_scale", [P, 1], F32)
        z_units = sb("z_units", [P, 1], F32)

        arena = sb("arena", [P, 28300], F32)
        at = [0]

        def take(parts, *dims):
            n = 1
            for d in dims:
                n *= d
            v = arena[0:parts, at[0]:at[0] + n]
            at[0] += n
            if len(dims) == 1:
                return v
            names = "abcd"[:len(dims)]
            return v.rearrange(f"z ({' '.join(names)}) -> z {' '.join(names)}", **dict(zip(names[1:], dims[1:])))

        xn = take(P, TT, D)
        xl = take(P, TT, D)
        kept = at[0]
        wh32 = take(P, KC, NG4)
        wx32 = wh32
        NW = 3
        w2_sb = [take(P, KC, P * R) for _ in range(NW)]
        bup, w1_sb = (w2_sb[2][:, 2 * i:2 * i + 2, :].rearrange("p a (b n) -> p (a b) n", b=2) for i in range(2))
        bias_u = take(P, WT, R)
        ft = take(P, R, 32)
        a2_n = take(P, KC, BR)
        a1_n = take(P, KC, 2, BR)
        b2_n = take(P, KC, 2, BR)
        a2_t = take(BR, D)
        cond_sb = take(NB, D)
        cond_l = take(NB, D)
        gam = take(NB, D)
        bet = take(NB, D)
        cn = take(NB, D)
        cT = take(P, KC, NB)
        condT = take(P, KC, NB)
        b1_sb = take(P, KC)
        brow = take(NCB, P)
        wmax = take(P, 4)
        wexp = take(P, 1)
        winv = take(P, 1)
        stats = take(NB, 6)
        mv = take(NB, 2)
        veps = take(NB, 1)
        sdev = take(NB, 1)
        rstd = take(NB, 1)
        newt = take(NB, 2)
        h0_t = take(P, 2, 8, 32)
        hidT = sb("hidT", [P, KC, NB], F32)

        ld_cond = sem("ld_cond")
        ld_small = sem("ld_small")
        ld_bias = sem("ld_bias")
        ld_w1 = sem("ld_w1")
        ld_wh = sem("ld_wh")
        ld_wx = sem("ld_wx")
        ld_bup = sem("ld_bup")
        ld_bias2 = sem("ld_bias2")
        ld_w2 = [sem(f"ld_w2_{i}") for i in range(NW)]
        ad_ps = sem("ad_ps")
        ad_zero = sem("ad_zero")
        ad_tr = sem("ad_tr")
        fac_ok = sem("fac_ok")
        fac_ps = sem("fac_ps")
        lane_ok = sem("lane_ok")
        ld_based = sem("ld_based")
        ident_zero = sem("ident_zero")
        ident_ok = sem("ident_ok")
        own_step = sem("own_step")
        ld_own = sem("ld_own")
        wx_ok = sem("wx_ok")
        ln_step = sem("ln_step")
        sdev_ok = sem("sdev_ok")
        cn_ok = sem("cn_ok")
        cT_ps = sem("cT_ps")
        cT_ok = sem("cT_ok")
        condT_ps = sem("condT_ps")
        condT_ok = sem("condT_ok")
        hid_ps = sem("hid_ps")
        hid_ok = sem("hid_ok")
        bup_ps = sem("bup_ps")
        bup_ok = sem("bup_ok")
        wmax_ok = sem("wmax_ok")
        wmax_all = sem("wmax_all")
        ws_step = sem("ws_step")
        whi_ok = sem("whi_ok")
        wlo_ok = sem("wlo_ok")
        bz_ok = sem("bz_ok")
        h0_zero = sem("h0_zero")
        h0_tr = sem("h0_tr")
        cond_l_ok = sem("cond_l_ok")
        h0_ps = sem("h0_ps")
        h0_ok = sem("h0_ok")

        w2_v = W2.rearrange("(c p) (w n) -> w p c n", p=P, n=P * R)
        x_v = x.rearrange("b (m t) d -> m b t d", t=TB)
        ld_xn = sem("ld_xn")
        xl_ok = sem("xl_ok")
        xT_ps = sem("xT_ps")

        def load_x(sp, m):
            for bt in range(NB):
                sp.dma_start(xn[TB * (bt % BPT):TB * (bt % BPT + 1), bt // BPT, :],
                             x_v[bass.ds(m & (NBLK - 1), 1), bt].rearrange("m t d -> (m t) d")).then_inc(ld_xn, 16)

        def x_lane(pool, m, tt):
            if tt == 0:
                pool.wait_ge(ld_xn, m * (16 * NB) + 16 * NB)
                if not isinstance(m, int) or m > 0:
                    pool.wait_ge(xT_ps, m * KC)
                pool.sem_inc(pace["pool"], 1)
            nc.gpsimd.tensor_copy(lane_view(xl[:, tt, :]), in_lanes(xn[:, tt, :])).then_inc(xl_ok, 1)

        with nc.Block() as block:
            @block.sync
            def _(sp):
                sp.dma_start(cond_sb, cond).then_inc(ld_cond, 16)
                sp.dma_start(gam, ln_gamma.partition_broadcast(NB)).then_inc(ld_small, 16)
                sp.dma_start(bet, ln_beta.partition_broadcast(NB)).then_inc(ld_small, 16)
                sp.dma_start(w1_sb, W1.rearrange("(c p) n -> p c n", p=P)).then_inc(ld_w1, 16)
                sp.dma_start(bup, base_up.rearrange("(c p) n -> p c n", p=P)).then_inc(ld_bup, 16)
                for q, rows in enumerate(lanes(Wh)):
                    sp.dma_start(wh32[32 * q:32 * q + 32], rows).then_inc(ld_wh, 16)
                for i in range(2):
                    sp.dma_start(w2_sb[i], w2_v[i]).then_inc(ld_w2[i], 16)
                sp.wait_ge(hid_ps, KC)
                sp.wait_ge(bup_ps, KC)
                sp.dma_start(w2_sb[2], w2_v[2]).then_inc(ld_w2[2], 16)
                for q, rows in enumerate(lanes(base_down)):
                    sp.dma_start(based[32 * q:32 * q + 32], rows).then_inc(ld_based, 16)
                with sp.Fori(1, WT // NW) as r:
                    for i in range(NW):
                        sp.wait_ge(ad_ps, r * NW + (i + 1 - NW))
                        sp.sem_inc(pace["sp"], 1)
                        sp.dma_start(w2_sb[i], w2_v[bass.ds(r * NW + i, 1)].rearrange("a p c n -> p (a c) n")
                                     ).then_inc(ld_w2[i], 16)
                sp.wait_ge(ad_ps, WT - NW)
                sp.dma_start(w2_sb[0], w2_v[WT - 1]).then_inc(ld_w2[0], 16)
                load_x(sp, 0)
                sp.wait_ge(ld_based, 16 * KC)

            @block.gpsimd
            def _(pool):
                nc.gpsimd.memset(ident[:], 0.0).then_inc(ident_zero, 1)
                pool.wait_ge(ident_zero, 1)
                nc.gpsimd.affine_select(out=ident[:], in_=ident[:], compare_op=ALU.not_equal, fill=1.0,
                                        base=0, pattern=[[-1, P]], channel_multiplier=1).then_inc(ident_ok, 1)
                nc.gpsimd.memset(own[0:BR], 1.0).then_inc(own_step, 1)
                pool.wait_ge(own_step, 1)
                nc.gpsimd.affine_select(out=own[0:BR], in_=own[0:BR], compare_op=ALU.is_ge, fill=0.0, base=0,
                                        pattern=[[-R, NB], [0, TB]], channel_multiplier=1).then_inc(own_step, 1)
                pool.wait_ge(own_step, 2)
                nc.gpsimd.affine_select(out=own[0:BR], in_=own[0:BR], compare_op=ALU.is_ge, fill=0.0, base=R - 1,
                                        pattern=[[R, NB], [0, TB]], channel_multiplier=-1).then_inc(own_step, 1)
                pool.wait_ge(own_step, 3)
                pool.dma_start(own[BR:2 * BR], own[0:BR]).then_inc(ld_own, 16)
                pool.wait_ge(wmax_ok, 5)
                nc.gpsimd.partition_all_reduce(wexp, winv, P, RMAX).then_inc(wmax_all, 1)
                pool.wait_ge(ld_own, 16)
                pool.wait_ge(wlo_ok, 2 * KC)
                pool.wait_ge(h0_ps, 1)
                for q, rows in enumerate(lanes(Wx)):
                    pool.dma_start(wx32[32 * q:32 * q + 32], rows).then_inc(ld_wx, 16)
                pool.wait_ge(ld_wx, 16 * KC)
                for tt in range(TT):
                    x_lane(pool, 0, tt)

            @block.vector
            def _(dve):
                nc.vector.memset(banks[2][:], 0.0)
                nc.vector.memset(banks[3][:], 0.0).then_inc(h0_zero, 1)
                dve.wait_ge(ld_cond, 16)
                nc.vector.tensor_copy(lane_view(cond_l), in_lanes(cond_sb)).then_inc(cond_l_ok, 1)
                nc.vector.bn_stats(stats, cond_sb).then_inc(ln_step, 1)
                dve.wait_ge(ln_step, 1)
                nc.vector.bn_aggr(mv, stats).then_inc(ln_step, 1)
                dve.wait_ge(ln_step, 2)
                nc.vector.tensor_scalar(veps, mv[:, 1:2], LN_EPS, None, ALU.add).then_inc(ln_step, 1)
                dve.wait_ge(sdev_ok, 1)
                nc.vector.reciprocal(rstd, sdev).then_inc(ln_step, 1)
                dve.wait_ge(ln_step, 4)
                nc.vector.tensor_scalar(newt[:, 0:1], rstd, rstd, veps, ALU.mult, ALU.mult).then_inc(ln_step, 1)
                dve.wait_ge(ln_step, 5)
                nc.vector.tensor_scalar(newt[:, 1:2], newt[:, 0:1], -0.5, 1.5, ALU.mult, ALU.add).then_inc(ln_step, 1)
                dve.wait_ge(ln_step, 6)
                nc.vector.tensor_scalar(rstd, rstd, newt[:, 1:2], None, ALU.mult).then_inc(ln_step, 1)
                dve.wait_ge(ln_step, 7)
                nc.vector.tensor_scalar(cn, cond_sb, mv[:, 0:1], rstd, ALU.subtract, ALU.mult).then_inc(ln_step, 1)
                dve.wait_ge(ln_step, 8)
                dve.wait_ge(ld_small, 16 * 2)
                nc.vector.tensor_tensor(cn, cn, gam, ALU.mult).then_inc(ln_step, 1)
                dve.wait_ge(ln_step, 9)
                nc.vector.tensor_tensor(cn, cn, bet, ALU.add).then_inc(cn_ok, 1)
                dve.wait_ge(condT_ps, 1)
                nc.vector.tensor_copy(condT, banks[1][:, 0:KC * NB].rearrange("p (c n) -> p c n", c=KC)).then_inc(condT_ok, 1)
                dve.wait_ge(cT_ps, 1)
                nc.vector.tensor_copy(cT, banks[0][:, 0:KC * NB].rearrange("p (c n) -> p c n", c=KC)).then_inc(cT_ok, 1)
                for lc in range(KC):
                    dve.wait_ge(bup_ps, lc + 1)
                    nc.vector.tensor_scalar(lane_view(baseu[:, lc, :]), in_lanes(banks[4 + lc][:]), H_SCALE, None,
                                            ALU.mult).then_inc(bup_ok, 1)
                dve.wait_ge(bup_ok, NW)
                for i in range(NW):
                    nc.vector.memset(banks[4 + i][:], 0.0).then_inc(ad_zero, 1)

                def take_tile(w):
                    j, q = w // KC, w % KC
                    if w > 0:
                        dve.wait_ge(fac_ok, w + min(w, KC) + max(w - 3 * KC, 0))
                    dve.wait_ge(ad_ps, w + 1)
                    nc.vector.transpose(ft.rearrange("p a b -> p (a b)"), banks[4 + w % NW][:, 0:32 * R]).then_inc(ad_tr, 1)
                    dve.wait_ge(ad_tr, w + 1)
                    for dst in ((a1_n[:, q, 0], a1_n[:, q, 1]), (b1_c[:, q],), (a2_n[:, q],), (b2_n[:, q, 0], b2_n[:, q, 1]))[j]:
                        nc.vector.tensor_tensor(dst.rearrange("p (b r) -> p r b", r=R), ft[:, :, 0:NB],
                                                bias_u[:, w, :].unsqueeze(2).to_broadcast([P, R, NB]),
                                                ALU.add).then_inc(fac_ok, 1)

                dve.wait_ge(ld_wh, 16 * KC)
                for kb in range(KC):
                    nc.vector.tensor_reduce(wmax[:, kb:kb + 1], wh32[:, kb, :], AX_X, ALU.max,
                                            apply_absolute_value=True).then_inc(wmax_ok, 1)
                dve.wait_ge(wmax_ok, 4)
                nc.vector.tensor_reduce(winv, wmax, AX_X, ALU.max).then_inc(wmax_ok, 1)
                dve.wait_ge(wmax_all, 1)
                nc.vector.tensor_scalar(wexp, wexp, MAX_FLOOR, None, ALU.max).then_inc(ws_step, 1)
                dve.wait_ge(ws_step, 1)
                nc.vector.tensor_scalar(wexp.bitcast(U32), wexp.bitcast(U32), EXPONENT_BITS, None,
                                        ALU.bitwise_and).then_inc(ws_step, 1)
                dve.wait_ge(ws_step, 2)
                nc.vector.reciprocal(winv, wexp).then_inc(ws_step, 1)
                dve.wait_ge(ws_step, 3)
                nc.vector.tensor_scalar(w_scale[:], winv, W_TOP, None, ALU.mult).then_inc(ws_step, 1)
                nc.vector.tensor_scalar(w_scale_h[:], winv, 0.5 * W_TOP, None, ALU.mult).then_inc(ws_step, 1)
                nc.vector.tensor_scalar(z_units[:], winv, W_TOP * H_SCALE, None, ALU.mult).then_inc(ws_step, 1)
                nc.vector.tensor_scalar(gate_scale[:], wexp, 1.0 / (W_TOP * H_SCALE), None, ALU.mult).then_inc(ws_step, 1)
                dve.wait_ge(ws_step, 7)
                dve.wait_ge(ld_bias2, 16)
                for kb in range(KC):
                    for lo, hi, sc in ((0, 3 * D, w_scale_h), (3 * D, 4 * D, w_scale)):
                        nc.vector.tensor_scalar(wh_hi[:, kb, lo:hi], wh32[:, kb, lo:hi], sc[:, 0:1], None,
                                                ALU.mult).then_inc(whi_ok, 1)
                    dve.wait_ge(whi_ok, 2 * kb + 2)
                    for lo, hi, sc in ((0, 3 * D, w_scale_h), (3 * D, 4 * D, w_scale)):
                        nc.vector.scalar_tensor_tensor(out=wh_lo[:, kb, lo:hi], in0=wh32[:, kb, lo:hi], scalar=sc[:, 0:1],
                                                       in1=wh_hi[:, kb, lo:hi], op0=ALU.mult,
                                                       op1=ALU.subtract).then_inc(wlo_ok, 1)
                    take_tile(kb)
                nc.vector.tensor_scalar(bias_z[:], banks[1][:, 64:64 + NCB], z_units[:, 0:1], None,
                                        ALU.mult).then_inc(bz_ok, 1)
                dve.wait_ge(bz_ok, 1)
                for half in range(2):
                    nc.vector.tensor_scalar(bias_z[:, 8 * half:8 * half + 6], bias_z[:, 8 * half:8 * half + 6], 0.5, None,
                                            ALU.mult).then_inc(bz_ok, 1)
                dve.wait_ge(h0_ps, 1)
                for half in range(2):
                    nc.vector.transpose(h0_t[:, half].rearrange("p a b -> p (a b)"), banks[2 + half][:, 0:256]).then_inc(h0_tr, 1)
                dve.wait_ge(h0_tr, 2)
                for half in range(2):
                    nc.vector.tensor_scalar(h0_z[:, 8 * half:8 * half + 6, :], h0_t[:, half, 0:6, 0:NB], z_units[:, 0:1], 0.5,
                                            ALU.mult, ALU.mult).then_inc(h0_ok, 1)
                    nc.vector.tensor_scalar(h0_z[:, 8 * half + 6:8 * half + 8, :], h0_t[:, half, 6:8, 0:NB],
                                            z_units[:, 0:1], None, ALU.mult).then_inc(h0_ok, 1)
                for w in range(KC, 2 * KC):
                    take_tile(w)
                dve.wait_ge(ld_wx, 16 * KC)
                for kb in range(KC):
                    take_tile(2 * KC + kb)
                    for g in range(G):
                        for half in range(2):
                            cb = 8 * half + 2 * g
                            src = wx32[:, kb, g * D:(g + 1) * D].rearrange("p (q h c l) -> p h c q l", q=KC, h=2, c=2)
                            nc.vector.tensor_scalar(wx_l[:, kb, cb:cb + 2, :].rearrange("p c (q l) -> p c q l", q=KC),
                                                    src[:, half], 0.5 if g < 3 else 1.0, None, ALU.mult).then_inc(wx_ok, 1)
                for w in range(3 * KC, WT):
                    take_tile(w)
                dve.wait_ge(fac_ps, 1)
                nc.vector.tensor_scalar(lane_view(a1_t[:]), in_lanes(banks[3][:]), H_SCALE, None, ALU.mult)
                dve.wait_ge(fac_ps, 2)
                nc.vector.tensor_copy(lane_view(a2_t), in_lanes(banks[0][0:BR, :])).then_inc(lane_ok, 1)
                dve.wait_ge(fac_ps, 3)
                nc.vector.tensor_copy(b2_t[:], banks[2][:])
                dve.wait_ge(fac_ps, 4)
                nc.vector.tensor_copy(a2_c[:], banks[1][:, 0:KC * BR].rearrange("p (k r) -> p k r", k=KC)).then_inc(lane_ok, 1)

            @block.scalar
            def _(act):
                with nc.allow_non_contiguous_dma("512 bias values, once"):
                    act.dma_start(b1_sb, bias1.rearrange("(c p) -> p c", p=P)).then_inc(ld_bias, 16)
                bv = b.rearrange("(g q h c p) -> h c g q p", g=G, q=KC, h=2, c=2)
                for h in range(2):
                    for c in range(2):
                        act.dma_start(brow[8 * h + c:8 * h + c + 7:2, :].rearrange("g (q p) -> g q p", q=KC),
                                      bv[h, c]).then_inc(ld_bias, 16)
                act.dma_start(bias_u, bias2.rearrange("(w p r) -> p w r", p=P, r=R)).then_inc(ld_bias2, 16)
                act.wait_ge(ln_step, 3)
                nc.scalar.activation(sdev, veps, ACT.Sqrt).then_inc(sdev_ok, 1)
                act.wait_ge(ld_bias, 16 * 5)
                for i in range(KC):
                    act.wait_ge(hid_ps, i + 1)
                    nc.scalar.activation(hidT[:, i, :], banks[0][:, 64 + i * NB:64 + (i + 1) * NB], ACT.Gelu,
                                         bias=b1_sb[:, i:i + 1]).then_inc(hid_ok, 1)
            @block.tensor
            def _(pe):
                pe.wait_ge(ident_ok, 1)
                pe.wait_ge(cond_l_ok, 1)
                for B in range(KC):
                    mm = nc.tensor.transpose(banks[1][:, B * NB:(B + 1) * NB], cond_l[:, B * P:(B + 1) * P], ident[0:NB, 0:NB])
                pe.wait_ge(ld_bias, 16 * 5)
                nc.tensor.transpose(banks[1][:, 64:64 + NCB], brow, ident[0:NCB, 0:NCB]).then_inc(condT_ps, 1)
                pe.wait_ge(ld_bup, 16)
                for lc in range(KC):
                    for kc in range(KC):
                        mm = nc.tensor.transpose(banks[4 + lc][:, kc * P:(kc + 1) * P], bup[:, kc, lc * P:(lc + 1) * P],
                                                 ident[:])
                    mm.then_inc(bup_ps, 1)
                pe.wait_ge(cn_ok, 1)
                for c in range(KC):
                    mm = nc.tensor.transpose(banks[0][:, c * NB:(c + 1) * NB], cn[:, c * P:(c + 1) * P], ident[0:NB, 0:NB])
                mm.then_inc(cT_ps, 1)
                pe.wait_ge(cT_ok, 1)
                pe.wait_ge(ld_w1, 16)
                for i in range(KC):
                    if i:
                        pe.wait_ge(hid_ok, i)
                    for c in range(KC):
                        mm = nc.tensor.matmul(banks[0][:, 64 + i * NB:64 + (i + 1) * NB], w1_sb[:, c, i * P:(i + 1) * P], cT[:, c, :],
                                              start=(c == 0), stop=(c == KC - 1))
                    mm.then_inc(hid_ps, 1)
                pe.wait_ge(condT_ok, 1)
                pe.wait_ge(ld_wh, 16 * KC)
                pe.wait_ge(h0_zero, 1)
                for half in range(2):
                    for kb in range(KC):
                        for q in range(KC):
                            mm = nc.tensor.matmul(
                                banks[2 + half][32 * q:32 * q + NB, 0:256], condT[:, kb, :],
                                wh32[:, kb, :].rearrange("p (g q c) -> p g q c", g=G, q=KC)[:, :, q, 64 * half:64 * half + 64],
                                start=(kb == 0), stop=(kb == KC - 1), tile_position=(0, 32 * q))
                mm.then_inc(h0_ps, 1)

                def tile(w, turn, i):
                    pe.wait_ge(ld_w2[i], turn * 16 + 16)
                    if isinstance(turn, int) and turn == 0:
                        pe.wait_ge(ad_zero, i + 1)
                    else:
                        pe.wait_ge(ad_tr, w + (1 - NW))
                    for c in range(KC):
                        for k in range(KC):
                            mm = nc.tensor.matmul(banks[4 + i][32 * k:32 * k + NB, 0:32 * R], hidT[:, c, :],
                                                  w2_sb[i][:, c, 32 * R * k:32 * R * (k + 1)].rearrange("p (u r) -> p r u", r=R),
                                                  start=(c == 0), stop=(c == KC - 1), tile_position=(0, 32 * k))
                    mm.then_inc(ad_ps, 1)

                pe.wait_ge(hid_ok, KC)
                for i in range(NW):
                    tile(i, 0, i)
                with pe.Fori(1, WT // NW) as turn:
                    for i in range(NW):
                        tile(turn * NW + i, turn, i)
                tile(WT - 1, WT // NW, 0)

                pe.wait_ge(bz_ok, 1)
                pe.wait_ge(h0_tr, 2)
                pe.wait_ge(fac_ok, 2 * KC)
                for k in range(KC):
                    mm = nc.tensor.transpose(banks[3][:, k * P:(k + 1) * P], a1_n[:, k].rearrange("p a b -> p (a b)"), ident[:])
                mm.then_inc(fac_ps, 1)
                pe.wait_ge(fac_ok, 4 * KC)
                for k in range(KC):
                    mm = nc.tensor.transpose(banks[0][0:BR, k * P:(k + 1) * P], a2_n[:, k], ident[:])
                mm.then_inc(fac_ps, 1)
                pe.wait_ge(fac_ok, 6 * KC)
                for k in range(KC):
                    mm = nc.tensor.transpose(banks[2][:, k * P:(k + 1) * P], b2_n[:, k].rearrange("p a b -> p (a b)"), ident[:])
                mm.then_inc(fac_ps, 1)
                pe.wait_ge(lane_ok, 1)
                for k in range(KC):
                    mm = nc.tensor.transpose(banks[1][:, k * BR:(k + 1) * BR], a2_t[:, k * P:(k + 1) * P], ident[0:BR, 0:BR])
                mm.then_inc(fac_ps, 1)

        at[0] = kept
        XS = 4
        xz = take(P, NCB, NB, 2 * TB)
        x2s = take(P, XS * KC, TOK)
        hs = take(P, KC, NB, 2 * TB)
        xT = take(P, KC, TOK)
        midT = take(P, KC, TOK)
        um = take(2 * BR, NB, TB)
        vm = take(2 * BR, NB, TB)
        y_t = take(P, P)
        y_n = [take(P, D) for _ in range(TT)]
        h_st = sb("h_st", [P, 2, KC, 2 * NB], F16)
        zt = [sb(f"zt{i}", [P, 8, 32], F32) for i in range(2)]
        u = [sb(f"u{i}", [P, 8, NB], F32) for i in range(2)]
        z = [sb(f"z{i}", [P, 8, NB], F32) for i in range(2)]
        gt = [sb(f"gt{i}", [P, 10, NB], F32) for i in range(2)]
        os_ = [sb(f"os{i}", [P, 2, NB], F32) for i in range(2)]
        parts = [sb(f"parts{i}", [P, 4, NB], F32) for i in range(2)]
        cell2 = [g[:, 8:10, :] for g in gt]
        xc = sb("xc", [P, NCB, NB], F32)
        hc = sb("hc", [P, 2, KC, NB], F32)
        tc = [sb(f"tc{i}", [P, 2, NB], F32) for i in range(2)]

        def pair(name):
            return [sem(f"{name}0"), sem(f"{name}1")]

        state_ok = sem("state_ok")
        z_ps = pair("z_ps")
        zt_ok = pair("zt_ok")
        u_ok = pair("u_ok")
        z_ok = pair("z_ok")
        gt_ok = pair("gt_ok")
        parts_ok = pair("parts_ok")
        xc_ok = sem("xc_ok")
        hs_ok = sem("hs_ok")
        cell_ok = pair("cell_ok")
        tc_ok = pair("tc_ok")
        h32_ok = pair("h32_ok")
        h_ok = pair("h_ok")
        proj_ps = sem("proj_ps")
        proj_ok = sem("proj_ok")
        h0_in = sem("h0_in")
        xT_ok = sem("xT_ok")
        um_ps = sem("um_ps")
        um_ok = sem("um_ok")
        mid_ps = sem("mid_ps")
        mid_ok = sem("mid_ok")
        vm_ps = sem("vm_ps")
        vm_ok = sem("vm_ok")
        out_ps = sem("out_ps")
        x2_ok = sem("x2_ok")
        y_add = sem("y_add")
        y_ps = sem("y_ps")
        y_ok = sem("y_ok")
        y_free = pair("y_free")
        st_y = sem("st_y")

        z_bank = banks[0:2]
        proj_bank = banks[2:4]
        mix_bank = banks[4:7]
        y_bank = banks[7]
        wh_v = [w[:].rearrange("p k (g q c) -> p k g q c", g=G, q=KC) for w in (wh_hi, wh_lo)]
        out_v = out.rearrange("b (m t) d -> m b t d", t=TB)
        x2s_t = x2s.rearrange("p c (b t) -> p (c b) t", t=TB)
        hs_t = hs.rearrange("p c b t -> p (c b) t")

        def mix_out(i):
            return mix_bank[i % 3]

        UM_AT, MID_AT, VM_AT, OUT_AT, MIX_END = 3, 4, 17, 18, 31
        TERMS = KC + 1

        def terms(base, s):
            return [i for i in range(TERMS * KC) if base + 2 * i // 3 == s]

        def last_step(base, k):
            return base + 2 * (TERMS * k + TERMS - 1) // 3

        with nc.Block() as block:
            @block.sync
            def _(sp):
                def store_y(n, tt):
                    sp.wait_ge(y_ok, n * (TT * KC) + (tt * KC + KC + 1))
                    sp.sem_inc(pace["sp"], 1)
                    for i in range(BPT):
                        sp.dma_start(out_v[bass.ds((n + NBLK - 1) & (NBLK - 1), 1), tt * BPT + i].rearrange(
                            "m t d -> (m t) d"), y_n[tt][TB * i:TB * (i + 1), :]).then_inc(st_y, 16)
                    sp.wait_ge(st_y, n * (16 * NB) + 16 * BPT * (tt + 1))
                    sp.sem_inc(y_free[tt], 1)

                for m in range(1, 4):
                    sp.wait_ge(xl_ok, TT * m)
                    load_x(sp, m)
                for tt in range(TT):
                    sp.sem_inc(y_free[tt], 1)
                with sp.Fori(0, NBLK) as n:
                    store_y(n, 0)
                    sp.wait_ge(xl_ok, n * TT + TT * 4)
                    sp.sem_inc(pace["sp"], 1)
                    load_x(sp, n + 4)
                    store_y(n, 1)
                for tt in range(TT):
                    store_y(NBLK, tt)
                sp.wait_ge(ld_xn, 16 * NB * (NBLK + 4))
                sp.wait_ge(st_y, 16 * NB * (NBLK + 1))

            @block.gpsimd
            def _(pool):
                def y_sum(n, k):
                    tt, B = k // KC, k % KC
                    if k == 0:
                        pool.wait_ge(hs_ok, n * TB + 2)
                    pool.wait_ge(y_ps, n * (TT * KC) + (k + 1))
                    nc.gpsimd.tensor_tensor(
                        y_t.rearrange("p (b t) -> p b t", t=TB),
                        hs_t[:, B * NB + tt * BPT:B * NB + (tt + 1) * BPT, bass.ds(((n + 1) & 1) * TB, TB)],
                        x2s_t[:, bass.ds(((n + 3) & (XS - 1)) * (KC * NB) + (B * NB + tt * BPT), BPT), :],
                        ALU.add).then_inc(y_add, 1)

                def keep_h(s, pos, t):
                    pool.wait_ge(h32_ok[0], t + 1)
                    pool.wait_ge(h32_ok[1], t + 1)
                    pool.sem_inc(pace["pool"], 1)
                    nc.gpsimd.tensor_copy(hs[:, :, :, bass.ds(pos, 1)].rearrange("p c b t -> p c (b t)"),
                                          hc[:, s & 1]).then_inc(hs_ok, 1)

                for m in range(1, 3):
                    for tt in range(TT):
                        x_lane(pool, m, tt)
                pool.wait_ge(state_ok, 7)
                pool.sem_inc(hs_ok, 2)
                with pool.Fori(0, NBLK) as n:
                    for s in range(TB):
                        if s % KC == 0:
                            y_sum(n, s // KC)
                        if s % KC == 2 and s // KC in (1, 3):
                            x_lane(pool, n + 3, s // (2 * KC))
                        keep_h(s, (n & 1) * TB + s, n * TB + s)
                for k in range(TT * KC):
                    y_sum(NBLK, k)

            @block.tensor
            def _(pe):
                def mix(m, s):
                    if s < 2:
                        for B in (2 * s, 2 * s + 1):
                            if B == 0:
                                pe.wait_ge(xl_ok, m * TT + TT)
                            if B < 3:
                                if not isinstance(m, int) or m > 0:
                                    pe.wait_ge(x2_ok, m * KC)
                            else:
                                pe.wait_ge(xT_ok, m * KC + 1)
                            for tt in range(TT):
                                mm = nc.tensor.transpose(mix_out(B)[:, tt * P:(tt + 1) * P],
                                                         xl[:, tt, B * P:(B + 1) * P], ident[:])
                            mm.then_inc(xT_ps, 1)
                    if s == UM_AT:
                        pe.wait_ge(xT_ok, m * KC + KC)
                        for B in range(KC):
                            part = slice(BR * (B % 2), BR * (B % 2) + BR)
                            mm = nc.tensor.matmul(mix_out(4)[part, 0:TOK], a2_c[:, B, :], xT[:, B, :],
                                                  start=(B < 2), stop=(B >= 2), tile_position=(0, BR * (B % 2)))
                        mm.then_inc(um_ps, 1)
                    for i in terms(MID_AT, s):
                        lc, term = i // TERMS, i % TERMS
                        if term == 0 and lc == 2:
                            pe.wait_ge(um_ok, m + 1)
                        if term == 0 and lc == 3:
                            pe.wait_ge(mid_ok, m * KC + 1)
                        if term < KC:
                            nc.tensor.matmul(mix_out(5 + lc)[:, 0:TOK], based[:, term, lc * P:(lc + 1) * P],
                                             xT[:, term, :], start=(term == 0), stop=False)
                        else:
                            if lc == 0:
                                pe.wait_ge(um_ok, m + 1)
                            nc.tensor.matmul(mix_out(5 + lc)[:, 0:TOK], b2_t[:, lc * P:(lc + 1) * P],
                                             um.rearrange("p b t -> p (b t)"), start=False,
                                             stop=True).then_inc(mid_ps, 1)
                    if s == VM_AT:
                        pe.wait_ge(mid_ok, m * KC + KC)
                        for lc in range(KC):
                            part = slice(BR * (lc % 2), BR * (lc % 2) + BR)
                            mm = nc.tensor.matmul(mix_out(9)[part, 0:TOK], b1_c[:, lc, :], midT[:, lc, :],
                                                  start=(lc < 2), stop=(lc >= 2), tile_position=(0, BR * (lc % 2)))
                        mm.then_inc(vm_ps, 1)
                    for i in terms(OUT_AT, s):
                        B, term = i // TERMS, i % TERMS
                        if term == 0 and B == 2:
                            pe.wait_ge(vm_ok, m + 1)
                        if term == 0 and B == 3:
                            pe.wait_ge(x2_ok, m * KC + 1)
                        if term < KC:
                            nc.tensor.matmul(mix_out(10 + B)[:, 0:TOK], baseu[:, term, B * P:(B + 1) * P],
                                             midT[:, term, :], start=(term == 0), stop=False)
                        else:
                            if B == 0:
                                pe.wait_ge(vm_ok, m + 1)
                            nc.tensor.matmul(mix_out(10 + B)[:, 0:TOK], a1_t[:, B * P:(B + 1) * P],
                                             vm.rearrange("p b t -> p (b t)"), start=False,
                                             stop=True).then_inc(out_ps, 1)

                def project(m, s):
                    turn, kb = s // KC, s % KC
                    if kb == 0 and (turn > 0 or not isinstance(m, int) or m > 0):
                        pe.wait_ge(proj_ok, m * NCB + 2 * turn)
                    if s == 0:
                        pe.wait_ge(x2_ok, m * KC + KC)
                    for i in range(2):
                        mm = nc.tensor.matmul(
                            proj_bank[i][:, 0:TOK], wx_l[:, kb, 2 * turn + i, :],
                            x2s[:, bass.ds((m & (XS - 1)) * KC + kb, 1), :].rearrange("p a t -> p (a t)"),
                            start=(kb == 0), stop=(kb == KC - 1))
                        if kb == KC - 1:
                            mm.then_inc(proj_ps, 1)

                def turn_y(n, k):
                    pe.wait_ge(y_add, n * (TT * KC) + (k + 1))
                    pe.wait_ge(y_ok, n * (TT * KC) + (k + 1))
                    nc.tensor.transpose(y_bank[:, 0:P], y_t, ident[:]).then_inc(y_ps, 1)

                def recur(parity, n_half, chunks, start=False, stop=False):
                    for kb in chunks:
                        for part in range(2):
                            for q in range(KC):
                                mm = nc.tensor.matmul(
                                    z_bank[n_half][32 * q:32 * q + 2 * NB, 0:256], h_st[:, parity, kb, :],
                                    wh_v[part][:, kb, :, q, 64 * n_half:64 * n_half + 64],
                                    start=(start and kb == chunks[0] and part == 0),
                                    stop=(stop and kb == chunks[-1] and part == 1), tile_position=(0, 32 * q))
                    return mm

                pe.sem_inc(y_ps, 1)
                for s in range(MIX_END):
                    mix(0, s)
                for s in range(TB):
                    project(0, s)
                    mix(1, s)
                pe.wait_ge(state_ok, 7)

                with pe.Fori(0, NBLK) as n:
                    for s in range(TB):
                        t = n * TB + s
                        par = s & 1
                        project(n + 1, s)
                        mix(n + 2, s)
                        if s % KC == 1:
                            turn_y(n, s // KC)
                        pe.wait_ge(h_ok[0], t + 1)
                        recur(par, 0, (0, 1), start=True)
                        recur(par, 1, (0,), start=True)
                        pe.wait_ge(h_ok[1], t + 1)
                        recur(par, 0, (2, 3), stop=True).then_inc(z_ps[0], 1)
                        recur(par, 1, (1,))
                        recur(par, 1, (2, 3), stop=True).then_inc(z_ps[1], 1)
                for k in range(TT * KC):
                    turn_y(NBLK, k)

            @block.scalar
            def _(act):
                gate_s = act.alloc_register("gate_s")
                proj_s = act.alloc_register("proj_s")
                act.reg_load(gate_s, gate_scale[0:1, 0:1].bitcast(U32))
                act.reg_load(proj_s, w_scale[0:1, 0:1].bitcast(U32))

                def mix(m, s):
                    for B in (2 * s, 2 * s + 1) if s < 2 else ():
                        act.wait_ge(xT_ps, m * KC + (B + 1))
                        nc.scalar.activation(xT[:, B, :], mix_out(B)[:, 0:TOK], ACT.Copy).then_inc(xT_ok, 1)
                    for lc in range(KC):
                        if s == last_step(MID_AT, lc):
                            act.wait_ge(mid_ps, m * KC + (lc + 1))
                            nc.scalar.activation(midT[:, lc, :], mix_out(5 + lc)[:, 0:TOK], ACT.Gelu).then_inc(mid_ok, 1)

                def take_projection(m, turn):
                    for i in range(2):
                        cb = 2 * turn + i
                        act.wait_ge(proj_ps, m * NCB + (cb + 1))
                        nc.scalar.activation(xz[:, cb, :, bass.ds((m & 1) * TB, TB)],
                                             proj_bank[i][:, 0:TOK].rearrange("p (b t) -> p b t", t=TB), ACT.Identity,
                                             bias=bias_z[:, cb:cb + 1], scale=proj_s).then_inc(proj_ok, 1)

                def xz_step(pos):
                    nc.scalar.activation(xc[:], xz[:, :, :, bass.ds(pos, 1)].rearrange("p a b t -> p a (b t)"),
                                         ACT.Copy).then_inc(xc_ok, 1)

                def take_y(n, k):
                    tt, B = k // KC, k % KC
                    act.wait_ge(y_ps, n * (TT * KC) + (k + 2))
                    if B == 0:
                        act.wait_ge(y_free[tt], n + 1)
                    nc.scalar.activation(y_n[tt].rearrange("a (q B p) -> a B q p", q=KC, B=KC)[:, B],
                                         y_bank[:, 0:P].rearrange("a (q p) -> a q p", q=KC), ACT.Copy,
                                         scale=1.0 / H_SCALE).then_inc(y_ok, 1)

                act.sem_inc(y_ok, 1)
                for s in range(MIX_END):
                    mix(0, s)
                for s in range(TB):
                    mix(1, s)
                    if s % KC == KC - 1:
                        take_projection(0, s // KC)

                with act.Fori(0, NBLK) as n:
                    for s in range(TB):
                        t = n * TB + s
                        if s > 0:
                            xz_step((n & 1) * TB + s)
                        else:
                            act.wait_ge(h0_in, 1)
                            xz_step((n & 1) * TB)
                        mix(n + 2, s)
                        if s % KC == KC - 1:
                            take_projection(n + 1, s // KC)
                        if s % KC == 1:
                            take_y(n, s // KC)
                        for half in range(2):
                            act.wait_ge(z_ok[half], t + 1)
                            nc.scalar.activation(gt[half][:, 0:8, :], z[half][:], ACT.Tanh, scale=gate_s).then_inc(gt_ok[half], 1)
                            act.wait_ge(gt_ok[half], t + 1)
                            nc.scalar.activation(os_[half][:], gt[half][:, 4:6, :], ACT.Copy, bias=0.5 * H_SCALE,
                                                 scale=0.5 * H_SCALE)
                            act.wait_ge(cell_ok[half], t + 1)
                            nc.scalar.activation(tc[half][:], cell2[half], ACT.Tanh, scale=0.5).then_inc(tc_ok[half], 1)
                for k in range(TT * KC):
                    take_y(NBLK, k)

            @block.vector
            def _(dve):
                def mix(m, s):
                    if s == UM_AT + 1:
                        dve.wait_ge(um_ps, m + 1)
                        nc.vector.tensor_tensor(um, mix_out(4)[:, 0:TOK].rearrange("p (b t) -> p b t", t=TB), own[:],
                                                ALU.mult).then_inc(um_ok, 1)
                    if s == VM_AT + 1:
                        dve.wait_ge(vm_ps, m + 1)
                        nc.vector.tensor_tensor(vm, mix_out(9)[:, 0:TOK].rearrange("p (b t) -> p b t", t=TB), own[:],
                                                ALU.mult).then_inc(vm_ok, 1)
                    for B in range(KC):
                        if s == last_step(OUT_AT, B):
                            dve.wait_ge(out_ps, m * KC + (B + 1))
                            nc.vector.scalar_tensor_tensor(
                                out=x2s[:, bass.ds((m & (XS - 1)) * KC + B, 1), :].rearrange("p a t -> p (a t)"),
                                in0=xT[:, B, :], scalar=2.0 * H_SCALE, in1=mix_out(10 + B)[:, 0:TOK], op0=ALU.mult,
                                op1=ALU.add).then_inc(x2_ok, 1)

                def to_lanes(half, t):
                    dve.wait_ge(z_ps[half], t + 1)
                    nc.vector.transpose(zt[half][:].rearrange("p a b -> p (a b)"),
                                        z_bank[half][:, 0:256]).then_inc(zt_ok[half], 1)

                def add_projection(half, t):
                    dve.wait_ge(zt_ok[half], t + 1)
                    nc.vector.tensor_tensor(u[half][:], zt[half][:, :, 0:NB],
                                            xc[:, 8 * half:8 * half + 8, :], ALU.add).then_inc(u_ok[half], 1)

                def add_low(half, t):
                    dve.wait_ge(u_ok[half], t + 1)
                    nc.vector.tensor_tensor(z[half][:], zt[half][:, :, NB:2 * NB], u[half][:],
                                            ALU.add).then_inc(z_ok[half], 1)

                def cell_parts(half, t):
                    dve.wait_ge(gt_ok[half], t + 1)
                    nc.vector.scalar_tensor_tensor(out=parts[half][:], in0=gt[half][:, 0:4, :], scalar=1.0,
                                                   in1=gt[half][:, 6:10, :], op0=ALU.add,
                                                   op1=ALU.mult).then_inc(parts_ok[half], 1)

                def new_cell(half, t):
                    dve.wait_ge(parts_ok[half], t + 1)
                    nc.vector.scalar_tensor_tensor(out=cell2[half], in0=parts[half][:, 2:4, :], scalar=0.5,
                                                   in1=parts[half][:, 0:2, :], op0=ALU.mult,
                                                   op1=ALU.add).then_inc(cell_ok[half], 1)

                def new_h(half, par, t):
                    ch = slice(2 * half, 2 * half + 2)
                    dve.wait_ge(tc_ok[half], t + 1)
                    nc.vector.tensor_tensor(h_st[:, 1 - par, ch, 0:NB], os_[half][:], tc[half][:], ALU.mult)
                    nc.vector.tensor_tensor(hc[:, par, ch, :], os_[half][:], tc[half][:],
                                            ALU.mult).then_inc(h32_ok[half], 1)

                def h_rest(half, par, t):
                    ch = slice(2 * half, 2 * half + 2)
                    dve.wait_ge(h32_ok[half], t + 1)
                    nc.vector.tensor_tensor(h_st[:, 1 - par, ch, NB:2 * NB], hc[:, par, ch, :],
                                            h_st[:, 1 - par, ch, 0:NB], ALU.subtract).then_inc(h_ok[half], 1)

                nc.vector.memset(h_st[:], 0.0).then_inc(state_ok, 1)
                for half in range(2):
                    nc.vector.memset(z_bank[half][:], 0.0).then_inc(state_ok, 1)
                nc.vector.memset(x2s[:, (XS - 1) * KC:XS * KC, :], 0.0).then_inc(state_ok, 1)
                nc.vector.memset(hs, 0.0).then_inc(state_ok, 1)
                for half in range(2):
                    nc.vector.memset(cell2[half], 0.0).then_inc(state_ok, 1)
                dve.wait_ge(state_ok, 7)
                for half in range(2):
                    dve.sem_inc(h_ok[half], 1)
                for m in range(2):
                    for s in range(MIX_END):
                        mix(m, s)
                dve.wait_ge(proj_ok, NCB)
                nc.vector.tensor_tensor(xz[:, :, :, 0], xz[:, :, :, 0], h0_z[:], ALU.add).then_inc(h0_in, 1)

                with dve.Fori(0, NBLK) as n:
                    for s in range(TB):
                        t = n * TB + s
                        par = s & 1
                        mix(n + 2, s)
                        dve.wait_ge(xc_ok, t + 1)
                        dve.wait_ge(hs_ok, t + 1)
                        to_lanes(0, t)
                        add_projection(0, t)
                        add_low(0, t)
                        to_lanes(1, t)
                        cell_parts(0, t)
                        add_projection(1, t)
                        new_cell(0, t)
                        add_low(1, t)
                        new_h(0, par, t)
                        cell_parts(1, t)
                        h_rest(0, par, t)
                        new_cell(1, t)
                        new_h(1, par, t)
                        h_rest(1, par, t)


_INS = ['x', 'cond_1024', 'L0_cond_base_up', 'L0_cond_base_down', 'L0_cond_ln_gamma', 'L0_cond_ln_beta',
        'L0_cond_W1', 'L0_cond_bias1', 'L0_cond_W2', 'L0_cond_bias2', 'L1_cond_Wx', 'L1_cond_Wh', 'L1_cond_b']
_OUTS = [((8, 1024, 512), 'float32')]


def kernel(**inputs):
    import numpy as _np
    import concourse.bacc as _bacc
    from concourse import mybir as _mybir
    from concourse.bass_utils import run_bass_kernel_spmd as _run

    nc = _bacc.Bacc("TRN2", target_bir_lowering=False, num_devices=1)
    arrays, args = {}, []
    for name in _INS:
        a = _np.ascontiguousarray(inputs[name])
        arrays[f"in_{name}_dram"] = a
        args.append(nc.dram_tensor(f"in_{name}_dram", a.shape, _mybir.dt.from_np(a.dtype), kind="ExternalInput").ap())
    for i, (shape, dtype) in enumerate(_OUTS):
        dt = _mybir.dt.from_np(_np.dtype(dtype))
        args.append(nc.dram_tensor(f"out_{i}_dram", shape, dt, kind="ExternalOutput").ap())
    lowrank_mixer_then_lstm(nc, *args)
    r = _run(nc, [arrays], core_ids=[0])
    got = tuple(r.results[0][f"out_{i}_dram"] for i in range(len(_OUTS)))
    return got[0]
```
